# Optimizing a Trainium2 kernel written in Bass

```python
import numpy as np
import jax
import jax.numpy as jnp

def _softmax(x, axis=-1):
    return jax.nn.softmax(x, axis=axis)

def _gelu(x):
    return jax.nn.gelu(x, approximate=True)

def _silu(x):
    return jax.nn.silu(x)

def _sigmoid(x):
    return jax.nn.sigmoid(x)

def _layernorm(x, axis=-1, eps=1e-05):
    m = jnp.mean(x, axis=axis, keepdims=True)
    v = jnp.var(x, axis=axis, keepdims=True)
    return (x - m) / jnp.sqrt(v + eps)

def _scatter_add(tgt, idx, src, axis=0):
    return tgt.at[idx].add(src)

def _segment_sum(src, seg, n):
    return jax.ops.segment_sum(src, seg, n)
kernel_name = 'mk_flamingo_gated_d1_seqx_r2_6bc718'

def setup_inputs(seed: int=0):
    np.random.seed(seed)
    _w = jnp.asarray

    def _rec_inputs():
        import jax
        import jax.numpy as jnp
        _rk = jax.random.key(seed)
        x = -0.0003929 + 0.9999 * jax.random.normal(jax.random.fold_in(_rk, 1), (8, 224, 1024), jnp.float32)
        _lenS = 224 - jax.random.randint(jax.random.fold_in(_rk, 7), (8,), 0, max(1, 224 // 4) + 1, jnp.int32)
        _lenS2 = 750 - jax.random.randint(jax.random.fold_in(_rk, 8), (8,), 0, max(1, 750 // 4) + 1, jnp.int32)
        _ctx_2048P = jax.random.normal(jax.random.fold_in(_rk, 11), (8, 16, 1024), jnp.float32)
        _ctx_2048c = jax.random.dirichlet(jax.random.fold_in(_rk, 511), 0.3 * jnp.ones((16,), jnp.float32), (8, 750))
        _ctx_2048t = jnp.einsum('bsk,bkd->bsd', _ctx_2048c, _ctx_2048P)
        _ctx_2048t = _ctx_2048t * jax.lax.rsqrt(jnp.mean(jnp.square(_ctx_2048t)) + 1e-12) * 0.953939
        ctx_2048 = -1.39393e-06 + 0.999914 * (_ctx_2048t + 0.3 * jax.random.normal(jax.random.fold_in(_rk, 611), (8, 750, 1024), jnp.float32))
        itok_BxS_0_1023 = jax.random.randint(jax.random.fold_in(_rk, 12), (8, 224), 0, 512, jnp.int32)
        _g = jax.random.normal(jax.random.fold_in(_rk, 9001), (2, 1), jnp.float32)
        _g = jnp.sign(_g) * jnp.maximum(jnp.abs(_g), 1.0) + (_g == 0) * 1.0
        g_xattn = _g[0]
        g_ffn = _g[1]
        return (x, ctx_2048, itok_BxS_0_1023, g_xattn, g_ffn)
    x, ctx_2048, itok_BxS_0_1023, g_xattn, g_ffn = _rec_inputs()

    def _L0_xattn_setup():
        import jax, jax.numpy as jnp
        import numpy as np
        B, Lq, Lk = (2, 2048, 512)
        Q_DIM, KV_DIM = (1024, 1024)
        H, HD = (16, 128)
        KVC, QC, R = (256, 384, 64)
        LOOKBACK = 8
        NEG = -1e+30

        def _rope(x, L):
            half = x.shape[-1] // 2
            inv_freq = 1.0 / 10000.0 ** (jnp.arange(half, dtype=jnp.float32) / half)
            ang = jnp.arange(L, dtype=jnp.float32)[:, None] * inv_freq
            cos, sin = (jnp.cos(ang), jnp.sin(ang))
            x1, x2 = (x[..., :half], x[..., half:])
            return jnp.concatenate([x1 * cos - x2 * sin, x1 * sin + x2 * cos], axis=-1)
        key = jax.random.key(seed)
        ks = jax.random.split(key, 11)

        def w(k, shape, fan_in):
            return jax.random.normal(k, shape, jnp.float32) / np.sqrt(fan_in).astype(np.float32)
        return {'q': jax.random.normal(ks[0], (B, Lq, Q_DIM), jnp.float32), 'kv': jax.random.normal(ks[1], (B, Lk, KV_DIM), jnp.float32), 'seg_id': jnp.sort(jax.random.randint(ks[2], (B, Lq), 0, Lk), axis=-1), 'W_kvc': w(ks[3], (KV_DIM, KVC), KV_DIM), 'W_dq': w(ks[4], (Q_DIM, QC), Q_DIM), 'W_uq': w(ks[5], (QC, H * HD), QC), 'W_qr': w(ks[6], (QC, H * R), QC), 'W_uk': w(ks[7], (KVC, H * HD), KVC), 'W_kr': w(ks[8], (KVC, R), KVC), 'W_uv': w(ks[9], (KVC, H * HD), KVC), 'W_o': w(ks[10], (H * HD, Q_DIM), H * HD)}
    _L0_xattn_all = _L0_xattn_setup()
    _L0_xattn_in = {k: v for k, v in _L0_xattn_all.items() if k in ('W_kvc', 'W_dq', 'W_uq', 'W_qr', 'W_uk', 'W_kr', 'W_uv', 'W_o')}
    del _L0_xattn_all

    def _L0_ffn_setup():
        import jax, jax.numpy as jnp
        import numpy as np
        TOP_K = 2
        key = jax.random.key(seed)
        ks = jax.random.split(key, 4)
        G, S, F, E, H = (4, 1024, 1024, 8, 1024)
        return {'x': jax.random.normal(ks[0], (G, S, F), dtype=jnp.float32), 'router_logits': jax.random.normal(ks[1], (F, E), dtype=jnp.float32) * 0.02, 'gating_einsum': jax.random.normal(ks[2], (E, 2, H, F), dtype=jnp.float32) * 0.02, 'linear': jax.random.normal(ks[3], (E, H, F), dtype=jnp.float32) * 0.02, 'per_expert_scale': jnp.ones((E,), dtype=jnp.float32), 'router_scale': jnp.ones((F,), dtype=jnp.float32)}
    _L0_ffn_all = _L0_ffn_setup()
    _L0_ffn_in = {k: v for k, v in _L0_ffn_all.items() if k in ('router_logits', 'gating_einsum', 'linear', 'per_expert_scale', 'router_scale')}
    del _L0_ffn_all
    return {'x': x, 'ctx_2048': ctx_2048, 'itok_BxS_0_1023': itok_BxS_0_1023, 'g_xattn': g_xattn, 'g_ffn': g_ffn, 'L0_xattn_W_kvc': _L0_xattn_in['W_kvc'], 'L0_xattn_W_dq': _L0_xattn_in['W_dq'], 'L0_xattn_W_uq': _L0_xattn_in['W_uq'], 'L0_xattn_W_qr': _L0_xattn_in['W_qr'], 'L0_xattn_W_uk': _L0_xattn_in['W_uk'], 'L0_xattn_W_kr': _L0_xattn_in['W_kr'], 'L0_xattn_W_uv': _L0_xattn_in['W_uv'], 'L0_xattn_W_o': _L0_xattn_in['W_o'], 'L0_ffn_router_logits': _L0_ffn_in['router_logits'], 'L0_ffn_gating_einsum': _L0_ffn_in['gating_einsum'], 'L0_ffn_linear': _L0_ffn_in['linear'], 'L0_ffn_per_expert_scale': _L0_ffn_in['per_expert_scale'], 'L0_ffn_router_scale': _L0_ffn_in['router_scale']}

def reference(x, ctx_2048, itok_BxS_0_1023, g_xattn, g_ffn, L0_xattn_W_kvc, L0_xattn_W_dq, L0_xattn_W_uq, L0_xattn_W_qr, L0_xattn_W_uk, L0_xattn_W_kr, L0_xattn_W_uv, L0_xattn_W_o, L0_ffn_router_logits, L0_ffn_gating_einsum, L0_ffn_linear, L0_ffn_per_expert_scale, L0_ffn_router_scale):
    import jax
    import jax.numpy as jnp

    def _L0_xattn_ref(q, kv, seg_id, W_kvc, W_dq, W_uq, W_qr, W_uk, W_kr, W_uv, W_o):
        import jax, jax.numpy as jnp
        import numpy as np
        B, Lq, Lk = (2, 2048, 512)
        Q_DIM, KV_DIM = (1024, 1024)
        H, HD = (16, 128)
        KVC, QC, R = (256, 384, 64)
        LOOKBACK = 8
        NEG = -1e+30

        def _rope(x, L):
            half = x.shape[-1] // 2
            inv_freq = 1.0 / 10000.0 ** (jnp.arange(half, dtype=jnp.float32) / half)
            ang = jnp.arange(L, dtype=jnp.float32)[:, None] * inv_freq
            cos, sin = (jnp.cos(ang), jnp.sin(ang))
            x1, x2 = (x[..., :half], x[..., half:])
            return jnp.concatenate([x1 * cos - x2 * sin, x1 * sin + x2 * cos], axis=-1)
        b, lq, _ = q.shape
        lk = kv.shape[1]
        kv_c = kv @ W_kvc
        q_c = q @ W_dq
        q_nope = (q_c @ W_uq).reshape(b, lq, H, HD).transpose(0, 2, 1, 3)
        q_rope = (q_c @ W_qr).reshape(b, lq, H, R).transpose(0, 2, 1, 3)
        k_nope = (kv_c @ W_uk).reshape(b, lk, H, HD)
        v = (kv_c @ W_uv).reshape(b, lk, H, HD)
        k_rope = kv_c @ W_kr
        q_rope = _rope(q_rope, lq)
        k_rope = _rope(k_rope, lk)
        scale = 1.0 / np.sqrt(HD + R).astype(np.float32)
        scores = (jnp.einsum('bhqd,bkhd->bhqk', q_nope, k_nope) + jnp.einsum('bhqr,bkr->bhqk', q_rope, k_rope)) * scale
        k_ids = jnp.arange(lk)[None, None, :]
        qs = seg_id[:, :, None]
        good = (k_ids <= qs) & (k_ids >= qs - LOOKBACK)
        scores = jnp.where(good[:, None, :, :], scores, NEG)
        attn = jax.nn.softmax(scores, axis=-1)
        out = jnp.einsum('bhqk,bkhd->bqhd', attn, v).reshape(b, lq, H * HD)
        return out @ W_o

    def _L0_ffn_ref(x, router_logits, gating_einsum, linear, per_expert_scale, router_scale):
        import jax, jax.numpy as jnp
        import numpy as np
        TOP_K = 2
        G, S, F = x.shape
        E = router_logits.shape[-1]
        H = linear.shape[1]
        k = TOP_K
        dtype = x.dtype
        var = jnp.mean(jnp.square(x.astype(jnp.float32)), axis=-1, keepdims=True)
        router_input = x * jax.lax.rsqrt(var + 1e-06).astype(dtype)
        root_size = jax.lax.rsqrt(jnp.array(F, dtype=dtype))
        router_input = router_input * root_size * router_scale.astype(dtype)
        logits = jnp.einsum('gsd,de->gse', router_input, router_logits.astype(dtype))
        logits32 = logits.astype(jnp.float32)
        probs = jax.nn.softmax(logits32, axis=-1)
        _, choices = jax.lax.approx_max_k(logits32, k=k)
        indicator = jax.nn.one_hot(choices, E, dtype=probs.dtype).sum(axis=-2)
        renorm = jnp.sum(indicator * probs, axis=-1, keepdims=True)
        renorm = jnp.where(renorm > 0.0, renorm, 1.0)
        weights = probs / renorm
        x_flat = x.reshape((-1, F))
        batch_size = G * S
        choices_flat = choices.ravel()
        xs_order = choices_flat.argsort()
        xs_reverse_argsort = xs_order.argsort()
        xs_indices = jnp.repeat(jnp.arange(batch_size), k)[xs_order]
        sorted_xs = x_flat[xs_indices, :]
        choices_oh = jax.nn.one_hot(choices, num_classes=E, dtype=jnp.int32)
        tokens_per_expert = jnp.sum(choices_oh, axis=(0, 1, 2))
        combine_weights = (choices_oh.astype(jnp.float32) * jnp.expand_dims(weights, axis=2)).sum(axis=-1).astype(weights.dtype)
        w_gate = jnp.transpose(gating_einsum, (0, 3, 1, 2)).reshape(E, F, 2 * H)
        gate_out = jax.lax.ragged_dot(sorted_xs, w_gate.astype(dtype), group_sizes=tokens_per_expert)
        gate_out = gate_out.reshape(gate_out.shape[0], 2, H)
        activation = jax.nn.gelu(gate_out[:, 0, :]) * gate_out[:, 1, :]
        expert_outputs = jax.lax.ragged_dot(activation, linear.astype(dtype), group_sizes=tokens_per_expert)
        expert_indices = jnp.repeat(jnp.arange(E), tokens_per_expert, total_repeat_length=expert_outputs.shape[0])
        expert_outputs = expert_outputs * per_expert_scale.astype(expert_outputs.dtype)[expert_indices, None]
        out = expert_outputs[xs_reverse_argsort].reshape((G, S, k, -1))
        out = jnp.einsum('blkd,blk->bld', out, combine_weights, preferred_element_type=out.dtype)
        return out
    x = x + jnp.tanh(g_xattn[0]) * _L0_xattn_ref(_layernorm(x, axis=-1), ctx_2048, itok_BxS_0_1023, L0_xattn_W_kvc, L0_xattn_W_dq, L0_xattn_W_uq, L0_xattn_W_qr, L0_xattn_W_uk, L0_xattn_W_kr, L0_xattn_W_uv, L0_xattn_W_o)
    x = x + jnp.tanh(g_ffn[0]) * _L0_ffn_ref(_layernorm(x, axis=-1), L0_ffn_router_logits, L0_ffn_gating_einsum, L0_ffn_linear, L0_ffn_per_expert_scale, L0_ffn_router_scale)
    return x

_drawn_inputs = setup_inputs


def setup_inputs(seed=0):
    import zlib

    import numpy as np

    out = dict(_drawn_inputs(seed))
    spreads = {'L0_ffn_per_expert_scale': (1.0, 0.6), 'L0_ffn_router_scale': (1.0, 0.2)}
    factors = {}
    for name, (base, spread) in spreads.items():
        noise = np.random.default_rng([zlib.crc32(name.encode()), seed]).standard_normal(out[name].shape)
        drawn = base * np.exp(spread * noise) if base else spread * noise
        out[name] = jnp.asarray(drawn.astype(out[name].dtype))
    for name, factor in factors.items():
        out[name] = (out[name] * factor).astype(out[name].dtype)
    return out
```

```python
from contextlib import ExitStack

import numpy as np
import concourse.bass as bass
from concourse import mybir

F32 = mybir.dt.float32
F32R = mybir.dt.float32r
I32 = mybir.dt.int32
U32 = mybir.dt.uint32
ALU = mybir.AluOpType
ACT = mybir.ActivationFunctionType
AX_X = mybir.AxisListType.X

P = 128
BATCH, LQ, D = 8, 224, 1024
LK = 750
NTOK = BATCH * LQ
NT = NTOK // P
FC = D // P
KVC, QC, R = 256, 384, 64
KW = KVC + R
H, HD = 16, 128
KT, KN = 6, LK // 6
QB = 448
BACK = 8
WIN = BACK + 1
QS = 7
GQ = 2 * QS
NG = LQ // GQ
GROUPS = BATCH * NG
RW = QS * H
SL = QS * WIN + 1
E, F, HID = 8, 1024, 1024
ST = 5
MAXT = 2 * NT + E - 1
NSUP = 2 * NTOK // (ST * P) + E
SLOTS = (MAXT + ST) * P
LN_EPS, RMS_EPS = 1e-5, 1e-6
SCALE = float(1.0 / np.sqrt(HD + R).astype(np.float32))
assert KN * KT == LK and SL * 2 == P and NG * GQ == LQ


def split_product(nc, out, left, right, start, stop):
    nc.tensor.matmul(out, left[0], right[0], start=start, stop=False)
    nc.tensor.matmul(out, left[0], right[1], start=False, stop=False)
    return nc.tensor.matmul(out, left[1], right[0], start=False, stop=stop)


class Count:

    def __init__(self, eng, sem, base=0):
        self.eng, self.sem, self.base, self.n = eng, sem, base, 0

    def mark(self, ins):
        ins.then_inc(self.sem, 1)
        self.n += 1

    def wait(self):
        self.eng.wait_ge(self.sem, self.base + self.n)


def program(nc, a, out, stop=9):
    with ExitStack() as whole:
        kv_rows = nc.dram_tensor("kv_rows", (BATCH * LK + BATCH, KW), F32).ap()
        qc_dram = nc.dram_tensor("qc_dram", (P, 3, NTOK), F32).ap()
        o_dram = nc.dram_tensor("o_dram", (P, H, NTOK), F32).ap()
        xn_rows = nc.dram_tensor("xn_rows", (NTOK + P, D), F32).ap()
        slot_info = nc.dram_tensor("slot_info", (SLOTS, 2), F32).ap()
        ident = whole.enter_context(nc.sbuf_tensor("ident", [P, P], F32))
        logits = whole.enter_context(nc.sbuf_tensor("logits", [P, NT, E], F32))
        gates = whole.enter_context(nc.sbuf_tensor("gates", [P, 2], F32))
        supers = whole.enter_context(nc.sbuf_tensor("supers", [1, NSUP + 1, 4], I32))
        squares = whole.enter_context(nc.sbuf_tensor("squares", [P, NT], F32))
        with ExitStack() as early:
            ahead = [early.enter_context(nc.sbuf_tensor(name, shape, F32)) for name, shape in
                     (("w_uq", [P, 3, H * HD]), ("w_qr", [P, 3, H * R]), ("w_ukT", [P, H, KVC]), ("w_uv", [P, 2, H * HD]))]
            ahead_in = early.enter_context(nc.semaphore("ahead_in"))
            keys_stage(nc, a, ident, gates, kv_rows, xn_rows, slot_info, ahead, ahead_in)
            if stop > 1:
                queries_stage(nc, a, ident, qc_dram)
            if stop > 2:
                attend_stage(nc, a, ident, ahead, ahead_in, kv_rows, qc_dram, o_dram)
        if stop > 3:
            project_stage(nc, a, ident, gates, logits, squares, o_dram, xn_rows, out)
        if stop > 4:
            route_stage(nc, a, gates, logits, squares, supers, slot_info)
        if stop > 5:
            experts_stage(nc, a, ident, supers, slot_info, xn_rows, out)


def keys_stage(nc, a, ident, gates, kv_rows, xn_rows, slot_info, ahead, ahead_in):
    with ExitStack() as ctx:
        sb = lambda name, shape, dt=F32: ctx.enter_context(nc.sbuf_tensor(name, shape, dt))
        ps = lambda name, shape: ctx.enter_context(nc.psum_tensor(name, shape, F32))
        sem = lambda name: ctx.enter_context(nc.semaphore(name))
        NBUF = 3
        ctx_t = sb("ctx_t", [P, NBUF, FC, KN])
        w_kv = sb("w_kv", [P, FC, KW])
        w_kvT = sb("w_kvT", [P, 2, D])
        w_kr = sb("w_kr", [P, 2, R])
        kcos = sb("kcos", [KN, KT, R])
        ksin = sb("ksin", [KN, KT, R])
        xcos = sb("xcos", [KN, 2, R])
        xsin = sb("xsin", [KN, 2, R])
        inv = sb("inv", [KN, 1])
        rows = sb("rows", [KN, 2, KW])
        means = sb("means", [P, 2, BATCH])
        mean_rows = sb("mean_rows", [2 * BATCH, P])
        zeros = sb("zeros", [P, D])
        fold_ps = ps("fold_ps", [P, 512])
        kv_ps = [ps(f"kv_ps{i}", [P, 512]) for i in range(2)]
        mean_ps = [ps(f"mean_ps{i}", [P, 512]) for i in range(2)]
        meanT_ps = ps("meanT_ps", [P, 512])

        weights_in = sem("k_weights_in")
        ctx_in = [sem(f"k_ctx_in{i}") for i in range(NBUF)]
        fold_done = sem("k_fold_done")
        fold_copied = sem("k_fold_copied")
        kv_done = sem("k_kv_done")
        kv_read = sem("k_kv_read")
        rows_ready = sem("k_rows_ready")
        rows_out = [sem(f"k_rows_out{i}") for i in range(2)]
        means_done = sem("k_means_done")
        mean_copied = sem("k_mean_copied")
        meanT_done = sem("k_meanT_done")
        meanT_copied = sem("k_meanT_copied")
        zeroed = sem("k_zeroed")
        fill_out = sem("k_fill_out")
        dve_own = sem("k_dve_own")
        gate_own = sem("k_gate_own")

        with nc.Block() as block:
            @block.sync
            def _(sp):
                for dst, src in ((w_kv[:, :, 0:KVC], a["w_kvc"]), (w_kvT[:], a["w_kvcT"]), (w_kr[:], a["w_kr"]),
                                 (kcos[:], a["kcos"]), (ksin[:], a["ksin"]), (ident[:], a["ident"]),
                                 (inv[:], a["inv"]), (gates[:], a["gates"])):
                    sp.dma_start(dst, src).then_inc(weights_in, 16)
                for t in range(NBUF):
                    sp.dma_start(ctx_t[:, t], a["ctxT"][t]).then_inc(ctx_in[t], 16)

                def load_ahead(t, slot):
                    sp.wait_ge(kv_done, t + 1)
                    sp.dma_start(ctx_t[:, slot], a["ctxT"][t + NBUF]).then_inc(ctx_in[slot], 16)

                with sp.Fori(0, BATCH - 1) as b:
                    for j in range(KT):
                        load_ahead(b * KT + j, j % NBUF)
                for j in range(KT - NBUF):
                    load_ahead((BATCH - 1) * KT + j, j % NBUF)
                sp.wait_ge(zeroed, 1)
                sp.dma_start(kv_rows[BATCH * LK:, KVC:], zeros[0:BATCH, 0:R]).then_inc(fill_out, 16)
                sp.dma_start(xn_rows[NTOK:, :], zeros[:]).then_inc(fill_out, 16)
                sp.dma_start(slot_info.rearrange("(t p) c -> p t c", p=P),
                             a["slot_fill"].rearrange("(t p) c -> p t c", p=P)).then_inc(fill_out, 16)
                sp.wait_ge(meanT_copied, 1)
                for k in range(2):
                    sp.dma_start(kv_rows[BATCH * LK:, k * P:(k + 1) * P],
                                 mean_rows[k * BATCH:(k + 1) * BATCH, :]).then_inc(fill_out, 16)
                sp.wait_ge(fill_out, 16 * 5)

            @block.gpsimd
            def _(pool):
                pool.memset(zeros[:], 0.0).then_inc(zeroed, 1)

            @block.tensor
            def _(pe):
                pe.sem_inc(means_done, 1)
                pe.wait_ge(weights_in, 16 * 8)
                for f in range(FC):
                    for k in range(2):
                        mm = nc.tensor.matmul(fold_ps[:, f * R:(f + 1) * R], w_kvT[:, k, f * P:(f + 1) * P],
                                              w_kr[:, k, :], start=(k == 0), stop=(k == 1))
                mm.then_inc(fold_done, 1)
                pe.wait_ge(fold_copied, 1)

                def mean_part(b, j):
                    pe.wait_ge(rows_ready, b * KT + (j + 1))
                    if j == 0:
                        pe.wait_ge(mean_copied, b + 1)
                    for k in range(2):
                        mm = nc.tensor.matmul(mean_ps[k][:, 0:1], rows[:, j % 2, k * P:(k + 1) * P], inv[:],
                                              start=(j == 0), stop=(j == KT - 1))
                    mm.then_inc(means_done, 1)

                with pe.Fori(0, BATCH) as b:
                    for j in range(KT):
                        pe.wait_ge(ctx_in[j % NBUF], b * (16 * KT // NBUF) + 16 * (j // NBUF + 1))
                        pe.wait_ge(kv_read, b * KT + max(j, 1))
                        for f in range(FC):
                            mm = nc.tensor.matmul(kv_ps[j % 2][0:KN, 0:KW], ctx_t[:, j % NBUF, f, :], w_kv[:, f, :],
                                                  start=(f == 0), stop=(f == FC - 1))
                        mm.then_inc(kv_done, 1)
                        if j:
                            mean_part(b, j - 1)
                    mean_part(b, KT - 1)
                pe.wait_ge(mean_copied, BATCH + 1)
                nc.tensor.transpose(meanT_ps[0:2 * BATCH, 0:P], means[:].rearrange("p k b -> p (k b)"),
                                    ident[:]).then_inc(meanT_done, 1)

            @block.vector
            def _(dve):
                dve.sem_inc(kv_read, 1)
                dve.sem_inc(mean_copied, 1)
                dve.wait_ge(fold_done, 1)
                nc.vector.tensor_copy(w_kv[:, :, KVC:KW],
                                      fold_ps[:].rearrange("p (f r) -> p f r", f=FC)).then_inc(fold_copied, 1)
                with dve.Fori(0, BATCH) as b:
                    own = Count(dve, dve_own, b * (KT * 2))
                    for j in range(KT):
                        dve.wait_ge(kv_done, b * KT + (j + 1))
                        dve.wait_ge(rows_out[j % 2], b * (16 * KT // 2) + 16 * (j // 2 + 1))
                        dve.wait_ge(means_done, b * KT + max(j, 1))
                        pr = kv_ps[j % 2][0:KN, KVC:KW]
                        own.mark(nc.vector.tensor_tensor(xcos[:, j % 2, :], pr, kcos[:, j, :], ALU.mult))
                        own.mark(nc.vector.tensor_tensor(xsin[:, j % 2, :], pr, ksin[:, j, :], ALU.mult))
                        nc.vector.tensor_copy(rows[:, j % 2, 0:KVC], kv_ps[j % 2][0:KN, 0:KVC]).then_inc(kv_read, 1)
                        own.wait()
                        half = R // 2
                        nc.vector.tensor_tensor(rows[:, j % 2, KVC:KVC + half], xcos[:, j % 2, 0:half],
                                                xsin[:, j % 2, half:R], ALU.subtract)
                        nc.vector.tensor_tensor(rows[:, j % 2, KVC + half:KW], xsin[:, j % 2, 0:half],
                                                xcos[:, j % 2, half:R], ALU.add).then_inc(rows_ready, 1)
                    dve.wait_ge(means_done, b * KT + KT + 1)
                    for k in range(2):
                        cp = nc.vector.tensor_copy(means[:, k, bass.ds(b, 1)], mean_ps[k][:, 0:1])
                    cp.then_inc(mean_copied, 1)
                dve.wait_ge(meanT_done, 1)
                nc.vector.tensor_copy(mean_rows[:], meanT_ps[0:2 * BATCH, 0:P]).then_inc(meanT_copied, 1)

            @block.scalar
            def _(act):
                for i in range(2):
                    act.sem_inc(rows_out[i], 16)
                act.wait_ge(weights_in, 16 * 8)
                nc.scalar.activation(gates[:], gates[:], ACT.Tanh).then_inc(gate_own, 1)
                w_uq, w_qr, w_ukT, w_uv = ahead
                with act.Fori(0, BATCH) as b:
                    for w, name, share in ((w_uq, "w_uq", H * HD // BATCH), (w_qr, "w_qr", H * R // BATCH),
                                           (w_uv, "w_uv", H * HD // BATCH)):
                        cut = bass.ds(b * share, share)
                        act.dma_start(w[:, :, cut], a[name][:, :, cut]).then_inc(ahead_in, 16)
                    cut = bass.ds(b * (H // BATCH), H // BATCH)
                    act.dma_start(w_ukT[:, cut, :], a["w_ukT"][:, cut, :]).then_inc(ahead_in, 16)
                    for j in range(KT):
                        act.wait_ge(rows_ready, b * KT + (j + 1))
                        act.dma_start(kv_rows[bass.ds(b * LK + j * KN, KN), :], rows[:, j % 2, :]).then_inc(rows_out[j % 2], 16)
                for i in range(2):
                    act.wait_ge(rows_out[i], 16 * (BATCH * KT // 2 + 1))


def queries_stage(nc, a, ident, qc_dram):
    with ExitStack() as ctx:
        sb = lambda name, shape, dt=F32: ctx.enter_context(nc.sbuf_tensor(name, shape, dt))
        ps = lambda name, shape: ctx.enter_context(nc.psum_tensor(name, shape, F32))
        sem = lambda name: ctx.enter_context(nc.semaphore(name))
        w_dq = sb("w_dq", [P, FC, QC])
        x_t = sb("x_t", [P, 2, D])
        xn_t = sb("xn_t", [P, 2, D])
        xnT = sb("xnT", [P, FC, NTOK])
        stats = sb("stats", [P, 2, 2, 6])
        mv = sb("mv", [P, 2, 2])
        rstd = sb("rstd", [P, 2])
        var = sb("var", [P, 2])
        spare = sb("spare", [P, 1])
        std = sb("std", [P, 2])
        qc_t = sb("qc_t", [P, 2, 3, QB])
        turn_ps = [ps(f"q_turn_ps{i}", [P, 4, P]) for i in range(2)]
        qc_ps = [ps(f"q_qc_ps{i}", [P, 512]) for i in range(3)]

        w_in = sem("q_w_in")
        x_in = [sem(f"q_x_in{i}") for i in range(2)]
        var_ready = sem("q_var_ready")
        std_ready = sem("q_std_ready")
        normed = sem("q_normed")
        turned = sem("q_turned")
        turned_copied = sem("q_turned_copied")
        qc_done = sem("q_qc_done")
        qc_copied = sem("q_qc_copied")
        qc_out = [sem(f"q_qc_out{i}") for i in range(2)]
        dve_own = sem("q_dve_own")

        with nc.Block() as block:
            @block.sync
            def _(sp):
                for i in range(2):
                    sp.dma_start(x_t[:, i], a["x"][i]).then_inc(x_in[i], 16)
                sp.dma_start(w_dq[:], a["w_dq"]).then_inc(w_in, 16)
                with sp.Fori(0, NT // 2 - 1) as t2:
                    for i in range(2):
                        sp.wait_ge(normed, t2 * 2 + (i + 1))
                        sp.dma_start(x_t[:, i], a["x"][t2 * 2 + (i + 2)]).then_inc(x_in[i], 16)
                for i in range(2):
                    sp.sem_inc(qc_out[i], 16)
                with sp.Fori(0, NTOK // QB // 2) as n2:
                    for i in range(2):
                        sp.wait_ge(qc_copied, n2 * 6 + (3 * (i + 1) + 1))
                        sp.dma_start(qc_dram[:, :, bass.ds(n2 * (2 * QB) + i * QB, QB)], qc_t[:, i]).then_inc(qc_out[i], 16)
                for i in range(2):
                    sp.wait_ge(qc_out[i], 16 * (NTOK // QB // 2 + 1))

            @block.vector
            def _(dve):
                dve.sem_inc(qc_copied, 1)
                with dve.Fori(0, NT // 2) as t2:
                    own = Count(dve, dve_own, t2 * 8)
                    for i in range(2):
                        dve.wait_ge(x_in[i], t2 * 16 + 16)
                        for h in range(2):
                            own.mark(nc.vector.bn_stats(stats[:, i, h, :], x_t[:, i, h * 512:(h + 1) * 512]))
                        own.wait()
                        nc.vector.tensor_copy(spare[:], stats[:, i, 0, 0:1])
                        own.mark(nc.vector.bn_aggr(mv[:, i, :], stats[:, i]))
                        own.wait()
                        nc.vector.tensor_scalar(var[:, i:i + 1], mv[:, i, 1:2], LN_EPS, None, ALU.add).then_inc(var_ready, 1)
                    for i in range(2):
                        dve.wait_ge(std_ready, t2 * 2 + (i + 1))
                        own.mark(nc.vector.reciprocal(rstd[:, i:i + 1], std[:, i:i + 1]))
                        own.wait()
                        dve.wait_ge(turned, t2 * 4 + 1)
                        nc.vector.tensor_scalar(xn_t[:, i, :], x_t[:, i, :], mv[:, i, 0:1], rstd[:, i:i + 1],
                                                ALU.subtract, ALU.mult).then_inc(normed, 1)
                with dve.Fori(0, NTOK // QB // 2) as n2:
                    for i in range(2):
                        for m in range(3):
                            dve.wait_ge(qc_done, n2 * 6 + (3 * i + m + 1))
                            if m == 0:
                                dve.wait_ge(qc_out[i], n2 * 16 + 16)
                            nc.vector.tensor_copy(qc_t[:, i, m, :], qc_ps[m][:, 0:QB]).then_inc(qc_copied, 1)

            @block.tensor
            def _(pe):
                pe.sem_inc(turned, 1)
                with pe.Fori(0, NT // 2) as t2:
                    for i in range(2):
                        pe.wait_ge(normed, t2 * 2 + (i + 1))
                        for g in range(2):
                            pe.wait_ge(turned_copied, t2 * 4 + (2 * i + g if i else 1))
                            for f in range(4):
                                c = g * 4 + f
                                mm = nc.tensor.transpose(turn_ps[g][:, f, :], xn_t[:, i, c * P:(c + 1) * P], ident[:])
                            mm.then_inc(turned, 1)
                pe.wait_ge(w_in, 16)
                pe.wait_ge(turned_copied, NT * 2 + 1)
                with pe.Fori(0, NTOK // QB) as n:
                    for m in range(3):
                        pe.wait_ge(qc_copied, n * 3 + 1)
                        for f in range(FC):
                            mm = nc.tensor.matmul(qc_ps[m][:, 0:QB], w_dq[:, f, m * P:(m + 1) * P],
                                                  xnT[:, f, bass.ds(n * QB, QB)], start=(f == 0), stop=(f == FC - 1))
                        mm.then_inc(qc_done, 1)

            @block.scalar
            def _(act):
                act.sem_inc(turned_copied, 1)
                with act.Fori(0, NT // 2) as t2:
                    for i in range(2):
                        act.wait_ge(var_ready, t2 * 2 + (i + 1))
                        nc.scalar.activation(std[:, i:i + 1], var[:, i:i + 1], ACT.Sqrt).then_inc(std_ready, 1)
                    for i in range(2):
                        for g in range(2):
                            act.wait_ge(turned, t2 * 4 + (2 * i + g + 2))
                            nc.scalar.copy(xnT[:, g * 4:g * 4 + 4, bass.ds(t2 * (2 * P) + i * P, P)], turn_ps[g][:]).then_inc(turned_copied, 1)


def attend_stage(nc, a, ident, ahead, ahead_in, kv_rows, qc_dram, o_dram):
    with ExitStack() as ctx:
        sb = lambda name, shape, dt=F32: ctx.enter_context(nc.sbuf_tensor(name, shape, dt))
        ps = lambda name, shape: ctx.enter_context(nc.psum_tensor(name, shape, F32))
        sem = lambda name: ctx.enter_context(nc.semaphore(name))
        NG_BUF = 4
        w_uq, w_qr, w_ukT, w_uv = ahead
        qc_t = sb("a_qc_t", [P, 3, LQ])
        q_nope = sb("q_nope", [P, 2, LQ])
        q_lat = [sb(f"q_lat{i}", [P, 2, LQ, H]) for i in range(2)]
        q_rot2 = sb("q_rot2", [2 * R, LQ, H])
        q_rot = [q_rot2[0:R], q_rot2[R:2 * R]]
        o_lat = sb("o_lat", [P, 2, H, LQ])
        o_t = sb("o_t", [P, 2, 2, LQ])
        qcos = sb("qcos", [2 * R, LQ])
        qsin = sb("qsin", [2 * R, LQ])
        by_cos = sb("by_cos", [2 * R, LQ])
        by_sin = sb("by_sin", [2 * R, LQ])
        window_i = sb("window_i", [P, GROUPS], I32)
        rows_i = sb("rows_i", [RW, 2 * GROUPS], I32)
        base = sb("base", [P, GROUPS])
        back = sb("back", [P, 1])
        keep = sb("keep", [P, 1])
        place_f = sb("place_f", [P, GROUPS])
        place = sb("place", [P, GROUPS], U32)
        place_of = sb("place_of", [P, NG_BUF], U32)
        seg_f = sb("seg_f", [RW, 2 * GROUPS])
        ma = sb("ma", [RW, SL])
        mb = sb("mb", [RW, SL])
        mc = sb("mc", [RW, SL])
        mask = sb("mask", [RW, 2, 2, SL])
        kv = sb("kv", [P, NG_BUF, KW])
        kvT = sb("kvT", [P, 2, P])
        krT2 = sb("krT2", [2 * R, P])
        krT = [krT2[0:R], krT2[R:2 * R]]
        score = sb("score", [RW, 2, 2, SL])
        top = sb("top", [RW, 2, 2])
        total = sb("total", [RW, 2, 2])
        share = sb("share", [RW, 2, 2])
        prob = sb("prob", [RW, 2, 2, SL])
        probT = sb("probT", [P, RW])
        nope_ps = ps("nope_ps", [P, 512])
        rot_ps = ps("rot_ps", [P, 512])
        lat_ps = ps("lat_ps", [P, 2, 256])
        turn_ps = ps("a_turn_ps", [P, 4, P])
        score_ps = ps("score_ps", [P, 512])
        probT_ps = ps("probT_ps", [P, 512])
        mix_ps = [ps(f"mix_ps{i}", [P, 2, 256]) for i in range(2)]

        consts_in = sem("a_consts_in")
        qc_in = sem("a_qc_in")
        nope_done, nope_read = sem("a_nope_done"), sem("a_nope_read")
        rot_done, rot_read = sem("a_rot_done"), sem("a_rot_read")
        lat_done, lat_read = sem("a_lat_done"), sem("a_lat_read")
        place_ready = sem("a_place_ready")
        kv_in = [sem(f"a_kv_in{i}") for i in range(NG_BUF)]
        turn_done, turn_read = sem("a_turn_done"), sem("a_turn_read")
        score_done, score_read = sem("a_score_done"), sem("a_score_read")
        mask_ready = sem("a_mask_ready")
        top_ready = sem("a_top_ready")
        exp_done = sem("a_exp_done")
        prob_ready = sem("a_prob_ready")
        probT_done, probT_read = sem("a_probT_done"), sem("a_probT_read")
        mix_done, mix_read = sem("a_mix_done"), sem("a_mix_read")
        o_out = [sem(f"a_o_out{i}") for i in range(2)]
        rot_own, soft_own, pool_own, set_own = sem("a_rot_own"), sem("a_soft_own"), sem("a_pool_own"), sem("a_set_own")
        HUV = H // 2

        def steps(eng, step):
            step(None, 0, 0, 0)
            with eng.Fori(0, BATCH // 2 - 1) as i:
                step(i * 2, i * 2 + 1, 0, 1)
                step(i * 2 + 1, i * 2 + 2, 1, 0)
            step(BATCH - 2, BATCH - 1, 0, 1)
            step(BATCH - 1, None, 1, 0)

        def heads_before(bg, bh):
            return (bh + 1) * H if bh is not None else (bg + 1) * H

        with nc.Block() as block:
            @block.sync
            def _(sp):
                sp.dma_start(qc_t[:], qc_dram[:, :, 0:LQ]).then_inc(qc_in, 16)
                for dst, src in ((window_i, "window"), (rows_i, "seg_rows"), (base, "base"), (back, "back"), (keep, "keep"),
                                 (ma, "ma"), (mb, "mb"), (mc, "mc"), (qcos, "qcos"), (qsin, "qsin")):
                    sp.dma_start(dst[:], a[src]).then_inc(consts_in, 16)
                for i in range(2):
                    sp.sem_inc(o_out[i], 16)

                def step(bg, bh, pg, ph):
                    if bh is not None and bg is None:
                        sp.wait_ge(rot_done, H)
                        sp.dma_start(qc_t[:], qc_dram[:, :, LQ:2 * LQ]).then_inc(qc_in, 16)
                        return
                    if bh is not None:
                        sp.wait_ge(rot_done, (bh + 1) * H + bg * HUV)
                        nxt = (bh + 1) * LQ if not isinstance(bh, int) or bh + 1 < BATCH else None
                        if nxt is not None:
                            sp.dma_start(qc_t[:], qc_dram[:, :, bass.ds(nxt, LQ)]).then_inc(qc_in, 16)
                    for q in range(HUV):
                        sp.wait_ge(nope_read, heads_before(bg, bh) + bg * HUV + (q + 2))
                        sp.wait_ge(rot_read, heads_before(bg, bh) + bg * HUV + (q + 2))
                        sp.dma_start(o_dram[:, 2 * q:2 * q + 2, bass.ds(bg * LQ, LQ)], o_t[:, q % 2]).then_inc(o_out[q % 2], 16)

                steps(sp, step)
                for i in range(2):
                    sp.wait_ge(o_out[i], 16 * (BATCH * HUV // 2 + 1))

            @block.gpsimd
            def _(pool):
                pool.wait_ge(place_ready, 1)
                gather_rows = kv_rows
                with pool.Fori(0, GROUPS // NG_BUF) as g4:
                    own = Count(pool, pool_own, g4 * (4 * NG_BUF))
                    for k in range(NG_BUF):
                        pool.wait_ge(mix_done, g4 * NG_BUF + (k + 1))
                        own.mark(pool.tensor_copy(place_of[:, k:k + 1], place[:, bass.ds(g4 * NG_BUF + k, 1)]))
                        own.wait()
                        pool.wait_ge(score_read, g4 * NG_BUF + (k + 1))
                        m = mask[:, k % 2]
                        wide = lambda t: t[:].unsqueeze(1).to_broadcast([RW, 2, SL])
                        seg = seg_f[:, bass.ds(g4 * (2 * NG_BUF) + 2 * k, 2)].unsqueeze(2).to_broadcast([RW, 2, SL])
                        own.mark(pool.tensor_tensor(m, wide(ma), seg, ALU.add))
                        pool.indirect_dma_start(kv[:, k, :], None, gather_rows,
                                                bass.IndirectOffsetOnAxis(place_of[:, k:k + 1], 0)).then_inc(kv_in[k], 16)
                        own.wait()
                        own.mark(pool.tensor_tensor(m, m, m, ALU.mult))
                        own.wait()
                        own.mark(pool.tensor_tensor(m, m, wide(mb), ALU.mult))
                        own.wait()
                        pool.tensor_tensor(m, m, wide(mc), ALU.add).then_inc(mask_ready, 1)

            @block.tensor
            def _(pe):
                pe.sem_inc(mix_done, NG_BUF)
                pe.wait_ge(ahead_in, 16 * 4 * BATCH)
                pe.wait_ge(qc_in, 16)

                def step(bg, bh, pg, ph):
                    uv0 = 0 if bg is None else bg * HUV
                    first = 0 if bg is None else bg * NG

                    def head(u):
                        n = bh * H + u
                        pe.wait_ge(nope_read, n + uv0 + 1)
                        for k in range(3):
                            mm = nc.tensor.matmul(nope_ps[:, 0:LQ], w_uq[:, k, u * HD:(u + 1) * HD], qc_t[:, k, :],
                                                  start=(k == 0), stop=(k == 2))
                        mm.then_inc(nope_done, 1)

                    def pair_rotary(v):
                        pe.wait_ge(rot_read, bh * H + 2 * v + uv0 + 1)
                        for k in range(3):
                            mm = nc.tensor.matmul(rot_ps[:, 0:LQ], w_qr[:, k, v * 2 * R:(v + 1) * 2 * R], qc_t[:, k, :],
                                                  start=(k == 0), stop=(k == 2))
                        mm.then_inc(rot_done, 2)

                    def head_latent(u):
                        n = bh * H + u
                        pe.wait_ge(nope_read, n + uv0 + 2)
                        pe.wait_ge(lat_read, n + 1)
                        for k in range(2):
                            mm = nc.tensor.matmul(lat_ps[:, k, 0:LQ], w_ukT[:, u, k * P:(k + 1) * P], q_nope[:, u % 2, :],
                                                  start=True, stop=True)
                        mm.then_inc(lat_done, 1)

                    def turn(u):
                        n = first + u
                        pe.wait_ge(kv_in[u % NG_BUF], bg * (16 * NG // NG_BUF) + 16 * (u // NG_BUF + 1))
                        pe.wait_ge(turn_read, n + 1)
                        for k in range(2):
                            nc.tensor.transpose(turn_ps[:, k, :], kv[:, u % NG_BUF, k * P:(k + 1) * P], ident[:])
                        nc.tensor.transpose(turn_ps[0:R, 2, :], kv[:, u % NG_BUF, KVC:KW], ident[:]).then_inc(turn_done, 1)

                    def scores(u):
                        n = first + u
                        pe.wait_ge(turn_read, n + 2)
                        pe.wait_ge(score_read, n + 2)
                        if u == 0:
                            pe.wait_ge(lat_read, (bg + 1) * H + 1)
                            pe.wait_ge(rot_read, (bg + 1) * H + bg * HUV + 1)
                        for s in range(2):
                            q0 = u * GQ + s * QS
                            o = score_ps[0:RW, s * SL:(s + 1) * SL]
                            for k in range(2):
                                nc.tensor.matmul(o, q_lat[pg][:, k, q0:q0 + QS, :].rearrange("p q h -> p (q h)"),
                                                 kvT[:, k, s * SL:(s + 1) * SL], start=(k == 0), stop=False)
                            mm = nc.tensor.matmul(o, q_rot[pg][:, q0:q0 + QS, :].rearrange("p q h -> p (q h)"),
                                                  krT[pg][:, s * SL:(s + 1) * SL], start=False, stop=True)
                        mm.then_inc(score_done, 1)

                    def turn_probs(u):
                        n = first + u
                        pe.wait_ge(prob_ready, n + 1)
                        pe.wait_ge(probT_read, n + 1)
                        nc.tensor.transpose(probT_ps[:, 0:RW], prob[:, u % 2].rearrange("p s c -> p (s c)"),
                                            ident[0:RW, 0:RW]).then_inc(probT_done, 1)

                    def mix(u):
                        n = first + u
                        pe.wait_ge(probT_read, n + 2)
                        pe.wait_ge(mix_read, n + 1)
                        for s in range(2):
                            for k in range(2):
                                mm = nc.tensor.matmul(mix_ps[s][:, k, 0:RW], kv[s * SL:(s + 1) * SL, u % NG_BUF, k * P:(k + 1) * P],
                                                      probT[s * SL:(s + 1) * SL, :], start=True, stop=True)
                        mm.then_inc(mix_done, 1)

                    if bh is not None and bg is not None:
                        pe.wait_ge(qc_in, bh * 16 + 16)
                    for u in range(H + 2 if bg is not None else H + 1):
                        if bh is not None and u < H:
                            head(u)
                        if bg is not None and u >= 2:
                            turn_probs(u - 2)
                        if bh is not None and u < H and u % 2:
                            pair_rotary(u // 2)
                        if bg is not None:
                            if u >= 2:
                                mix(u - 2)
                            if 1 <= u < NG + 1:
                                scores(u - 1)
                            if u < NG:
                                turn(u)
                        if bh is not None and 1 <= u < H + 1:
                            head_latent(u - 1)
                    if bg is None:
                        return
                    pe.wait_ge(mix_read, first + (NG + 1))
                    for h in range(H):
                        bank, done, read = ((nope_ps, nope_done, nope_read), (rot_ps, rot_done, rot_read))[h % 2]
                        pe.wait_ge(read, heads_before(bg, bh) + uv0 + (h // 2 + 1))
                        for k in range(2):
                            mm = nc.tensor.matmul(bank[:, 0:LQ], w_uv[:, k, h * HD:(h + 1) * HD], o_lat[:, k, h, :],
                                                  start=(k == 0), stop=(k == 1))
                        mm.then_inc(done, 1)

                steps(pe, step)

            @block.scalar
            def _(act):
                act.sem_inc(nope_read, 1)
                act.sem_inc(lat_read, 1)
                act.sem_inc(mix_read, 1)

                def step(bg, bh, pg, ph):
                    uv0 = 0 if bg is None else bg * HUV
                    first = 0 if bg is None else bg * NG
                    for u in range(H + 2 if bg is not None else H + 1):
                        if bh is not None and u < H:
                            act.wait_ge(nope_done, bh * H + uv0 + (u + 1))
                            nc.scalar.copy(q_nope[:, u % 2, :], nope_ps[:, 0:LQ]).then_inc(nope_read, 1)
                        if bg is not None and u >= 2:
                            w = u - 2
                            act.wait_ge(mix_done, first + (w + 1 + NG_BUF))
                            for s in range(2):
                                q0 = w * GQ + s * QS
                                cp = nc.scalar.copy(o_lat[:, :, :, q0:q0 + QS].rearrange("p k h q -> p k q h"),
                                                          mix_ps[s][:, :, 0:RW].rearrange("p k (q h) -> p k q h", h=H))
                            cp.then_inc(mix_read, 1)
                        if bg is not None and 1 <= u < NG + 1:
                            w = u - 1
                            act.wait_ge(top_ready, first + (w + 1))
                            for s in range(2):
                                ex = nc.scalar.activation(prob_raw(w)[:, s, :], score[:, w % 2, s, :], ACT.Exp,
                                                          bias=top[:, w % 2, s:s + 1], scale=SCALE,
                                                          accum_out=total[:, w % 2, s:s + 1])
                            ex.then_inc(exp_done, 1)
                        if bh is not None and 1 <= u < H + 1:
                            w = u - 1
                            act.wait_ge(lat_done, bh * H + (w + 1))
                            nc.scalar.copy(q_lat[ph][:, :, :, w], lat_ps[:, :, 0:LQ]).then_inc(lat_read, 1)
                    if bg is None:
                        return
                    for q in range(HUV):
                        act.wait_ge(nope_done, heads_before(bg, bh) + uv0 + (q + 1))
                        act.wait_ge(o_out[q % 2], bg * (16 * HUV // 2) + 16 * (q // 2 + 1))
                        nc.scalar.copy(o_t[:, q % 2, 0, :], nope_ps[:, 0:LQ]).then_inc(nope_read, 1)

                def prob_raw(w):
                    return score[:, w % 2]

                steps(act, step)

            @block.vector
            def _(dve):
                dve.sem_inc(rot_read, 1)
                dve.sem_inc(turn_read, 1)
                dve.sem_inc(score_read, 2)
                dve.sem_inc(probT_read, 1)
                dve.wait_ge(consts_in, 16 * 10)
                own = Count(dve, set_own)
                own.mark(nc.vector.tensor_copy(place_f[:], window_i[:]))
                own.mark(nc.vector.tensor_copy(seg_f[:], rows_i[:]))
                own.wait()
                own.mark(nc.vector.tensor_scalar(place_f[:], place_f[:], -1000.0, 2000.0, ALU.max, ALU.min))
                own.mark(nc.vector.tensor_scalar(seg_f[:], seg_f[:], -1000.0, 2000.0, ALU.max, ALU.min))
                own.wait()
                own.mark(nc.vector.tensor_scalar(place_f[:], place_f[:], back[:], 0.0, ALU.add, ALU.max))
                own.wait()
                own.mark(nc.vector.tensor_scalar(place_f[:], place_f[:], float(LK - 1), keep[:], ALU.min, ALU.mult))
                own.wait()
                nc.vector.tensor_tensor(place[:], place_f[:], base[:], ALU.add).then_inc(place_ready, 1)

                def step(bg, bh, pg, ph):
                    uv0 = 0 if bg is None else bg * HUV
                    first = 0 if bg is None else bg * NG
                    rot = Count(dve, rot_own, bh * (5 * H // 2)) if bh is not None else None
                    soft = Count(dve, soft_own, bg * (2 * NG)) if bg is not None else None
                    for u in range(H + 2 if bg is not None else H):
                        if bg is not None and u >= 2:
                            w = u - 2
                            dve.wait_ge(exp_done, first + (w + 1))
                            soft.mark(nc.vector.reciprocal(share[:, w % 2], total[:, w % 2]))
                            soft.wait()
                            nc.vector.tensor_tensor(prob[:, w % 2], score[:, w % 2],
                                                    share[:, w % 2].unsqueeze(2).to_broadcast([RW, 2, SL]),
                                                    ALU.mult).then_inc(prob_ready, 1)
                            dve.wait_ge(probT_done, first + (w + 1))
                            dve.wait_ge(mix_done, first + (w + NG_BUF))
                            nc.vector.tensor_copy(probT[:], probT_ps[:, 0:RW]).then_inc(probT_read, 1)
                        if bh is not None and u < H and u % 2:
                            v, hf = u // 2, R // 2
                            dve.wait_ge(rot_done, bh * H + uv0 + (2 * v + 2))
                            rot.mark(nc.vector.tensor_tensor(by_cos[:], rot_ps[:, 0:LQ], qcos[:], ALU.mult))
                            for to in range(4):
                                at, of = slice(to * hf, (to + 1) * hf), slice((to ^ 1) * hf, ((to ^ 1) + 1) * hf)
                                rot.mark(nc.vector.tensor_tensor(by_sin[at], rot_ps[of, 0:LQ], qsin[of], ALU.mult))
                            rot.wait()
                            nc.vector.tensor_tensor(q_rot[ph][:, :, 2 * v], by_cos[0:R], by_sin[0:R], ALU.add)
                            nc.vector.tensor_tensor(q_rot[ph][:, :, 2 * v + 1], by_cos[R:2 * R], by_sin[R:2 * R],
                                                    ALU.add).then_inc(rot_read, 2)
                        if bg is None:
                            continue
                        if 1 <= u < NG + 1:
                            w = u - 1
                            dve.wait_ge(score_done, first + (w + 1))
                            dve.wait_ge(mask_ready, first + (w + 1))
                            nc.vector.scalar_tensor_tensor(
                                score[:, w % 2].rearrange("p s c -> p (s c)"), mask[:, w % 2].rearrange("p s c -> p (s c)"), 0.0,
                                score_ps[0:RW, 0:2 * SL], ALU.min, ALU.add).then_inc(score_read, 1)
                            dve.wait_ge(score_read, first + (w + 3))
                            soft.mark(nc.vector.tensor_reduce(share[:, w % 2], score[:, w % 2], AX_X, ALU.max))
                            soft.wait()
                            nc.vector.tensor_scalar(top[:, w % 2], share[:, w % 2], -SCALE, None,
                                                    ALU.mult).then_inc(top_ready, 1)
                        if u < NG:
                            dve.wait_ge(turn_done, first + (u + 1))
                            if u:
                                dve.wait_ge(score_done, first + u)
                            nc.vector.tensor_copy(kvT[:], turn_ps[:, 0:2, :])
                            nc.vector.tensor_copy(krT[pg], turn_ps[0:R, 2, :]).then_inc(turn_read, 1)
                    if bg is None:
                        return
                    for q in range(HUV):
                        dve.wait_ge(rot_done, heads_before(bg, bh) + uv0 + (q + 1))
                        dve.wait_ge(o_out[q % 2], bg * (16 * HUV // 2) + 16 * (q // 2 + 1))
                        nc.vector.tensor_copy(o_t[:, q % 2, 1, :], rot_ps[:, 0:LQ]).then_inc(rot_read, 1)

                steps(dve, step)


def project_stage(nc, a, ident, gates, logits, squares, o_dram, xn_rows, out):
    with ExitStack() as ctx:
        sb = lambda name, shape, dt=F32: ctx.enter_context(nc.sbuf_tensor(name, shape, dt))
        ps = lambda name, shape: ctx.enter_context(nc.psum_tensor(name, shape, F32))
        sem = lambda name: ctx.enter_context(nc.semaphore(name))
        w_o = sb("w_o", [P, H, D])
        router = sb("router", [P, FC, E])
        router_scale = sb("router_scale", [P, FC])
        o_t = sb("p_o_t", [P, 2, H, P])
        x_t = sb("p_x_t", [P, 2, D])
        x1_t = sb("x1_t", [P, 2, D])
        xn_t = sb("p_xn_t", [P, 2, D])
        xnT = sb("p_xnT", [P, FC, P])
        sq = sb("p_sq", [P, 2, D])
        zeros = sb("p_zeros", [P, D])
        stats = sb("p_stats", [P, 2, 6])
        mv = sb("p_mv", [P, 2])
        spare = sb("p_spare", [P, 1])
        var = sb("p_var", [P, 1])
        std = sb("p_std", [P, 1])
        rstd = sb("p_rstd", [P, 1])
        attn_ps = [[ps(f"attn_ps{i}{h}", [P, 512]) for h in range(2)] for i in range(2)]
        turn_ps = [ps(f"p_turn_ps{i}", [P, 4, P]) for i in range(2)]
        logit_ps = ps("logit_ps", [P, 512])

        weights_in = sem("p_weights_in")
        consts_in = sem("p_consts_in")
        o_in = [sem(f"p_o_in{i}") for i in range(2)]
        x_in = [sem(f"p_x_in{i}") for i in range(2)]
        attn_done = sem("p_attn_done")
        x1_half = sem("p_x1_half")
        var_ready = sem("p_var_ready")
        std_ready = sem("p_std_ready")
        normed = sem("p_normed")
        turned, turned_copied = sem("p_turned"), sem("p_turned_copied")
        logits_done, logits_read = sem("p_logits_done"), sem("p_logits_read")
        scaled = sem("p_scaled")
        zeroed = sem("p_zeroed")
        rows_out = [sem(f"p_rows_out{i}") for i in range(2)]
        fill_out = sem("p_fill_out")
        own_sem = sem("p_dve_own")
        out_rows = out.rearrange("(t h) c -> t (h c)", h=2)

        LAST = NT // 2 - 1

        with nc.Block() as block:
            @block.sync
            def _(sp):
                sp.sem_inc(rows_out[0], 32)
                sp.sem_inc(rows_out[1], 32)
                sp.dma_start(router[:], a["router"]).then_inc(consts_in, 16)
                sp.dma_start(router_scale[:], a["router_scale"]).then_inc(consts_in, 16)
                sp.dma_start(o_t[:, 0], o_dram[:, :, 0:P]).then_inc(o_in[0], 16)
                for q in range(4):
                    if q:
                        sp.wait_ge(weights_in, 16 * q)
                    sp.dma_start(w_o[:, q * 4:q * 4 + 4], a["w_o"][:, q * 4:q * 4 + 4]).then_inc(weights_in, 16)
                sp.dma_start(x_t[:, 0], a["x"][0]).then_inc(x_in[0], 16)
                sp.dma_start(o_t[:, 1], o_dram[:, :, P:2 * P]).then_inc(o_in[1], 16)
                sp.dma_start(x_t[:, 1], a["x"][1]).then_inc(x_in[1], 16)
                sp.wait_ge(zeroed, 1)
                sp.dma_start(out_rows[NTOK:, :], zeros[:]).then_inc(fill_out, 16)

                def tile(t, i):
                    sp.wait_ge(normed, t + 1)
                    sp.dma_start(out_rows[bass.ds(t * P, P), :], x1_t[:, i]).then_inc(rows_out[i], 16)
                    sp.dma_start(xn_rows[bass.ds(t * P, P), :], xn_t[:, i]).then_inc(rows_out[i], 16)
                    if not isinstance(t, int) or t + 2 < NT:
                        sp.dma_start(x_t[:, i], a["x"][t + 2]).then_inc(x_in[i], 16)
                        sp.dma_start(o_t[:, i], o_dram[:, :, bass.ds((t + 2) * P, P)]).then_inc(o_in[i], 16)

                with sp.Fori(0, LAST) as j:
                    tile(j * 2, 0)
                    tile(j * 2 + 1, 1)
                tile(NT - 2, 0)
                tile(NT - 1, 1)
                for i in range(2):
                    sp.wait_ge(rows_out[i], 32 * (NT // 2 + 1))
                sp.wait_ge(fill_out, 16)

            @block.gpsimd
            def _(pool):
                pool.memset(zeros[:], 0.0).then_inc(zeroed, 1)

            @block.tensor
            def _(pe):
                pe.wait_ge(scaled, FC)

                def attn(t, i, m, turned_tile=None):
                    pe.wait_ge(o_in[i], m * 16 + 16)
                    pe.wait_ge(x1_half, t * 2 + 1)
                    for k in range(H):
                        if isinstance(t, int) and t == 0 and k % 4 == 0:
                            pe.wait_ge(weights_in, 16 * (k // 4 + 1))
                        if k == H // 2 and turned_tile is not None:
                            turn(turned_tile, 1 - i)
                        for h in range(2):
                            mm = nc.tensor.matmul(attn_ps[i][h][:], o_t[:, i, k, :], w_o[:, k, h * 512:(h + 1) * 512],
                                                  start=(k == 0), stop=(k == H - 1))
                    mm.then_inc(attn_done, 1)

                def turn(t, i):
                    pe.wait_ge(normed, t + 1)
                    for g in range(2):
                        pe.wait_ge(turned_copied, t * 2 + (g + 1))
                        for f in range(4):
                            c = g * 4 + f
                            mm = nc.tensor.transpose(turn_ps[g][:, f, :], xn_t[:, i, c * P:(c + 1) * P], ident[:])
                        mm.then_inc(turned, 1)

                def route(t):
                    pe.wait_ge(turned_copied, t * 2 + 4)
                    pe.wait_ge(logits_read, t + 1)
                    for f in range(FC):
                        mm = nc.tensor.matmul(logit_ps[:, 0:E], xnT[:, f, :], router[:, f, :], start=(f == 0), stop=(f == FC - 1))
                    mm.then_inc(logits_done, 1)

                pe.sem_inc(logits_done, 1)
                attn(0, 0, 0)
                with pe.Fori(0, LAST) as j:
                    attn(j * 2 + 1, 1, j, j * 2)
                    route(j * 2)
                    attn(j * 2 + 2, 0, j + 1, j * 2 + 1)
                    route(j * 2 + 1)
                attn(NT - 1, 1, LAST, NT - 2)
                route(NT - 2)
                turn(NT - 1, 1)
                route(NT - 1)

            @block.vector
            def _(dve):
                dve.sem_inc(x1_half, 3)
                dve.sem_inc(logits_read, 1)
                dve.wait_ge(consts_in, 32)
                for f in range(FC):
                    nc.vector.tensor_scalar(router[:, f, :], router[:, f, :], router_scale[:, f:f + 1], None,
                                            ALU.mult).then_inc(scaled, 1)

                def norm(t, i, m):
                    own = Count(dve, own_sem, t * 4)
                    dve.wait_ge(attn_done, t + 1)
                    dve.wait_ge(x_in[i], m * 16 + 16)
                    dve.wait_ge(rows_out[i], m * 32 + 32)
                    for h in range(2):
                        cut = slice(h * 512, (h + 1) * 512)
                        nc.vector.scalar_tensor_tensor(x1_t[:, i, cut], attn_ps[i][h][:], gates[:, 0:1], x_t[:, i, cut],
                                                       ALU.mult, ALU.add).then_inc(x1_half, 1)
                    dve.wait_ge(x1_half, t * 2 + 5)
                    for h in range(2):
                        own.mark(nc.vector.bn_stats(stats[:, h, :], x1_t[:, i, h * 512:(h + 1) * 512]))
                    own.wait()
                    nc.vector.tensor_copy(spare[:], stats[:, 0, 0:1])
                    own.mark(nc.vector.bn_aggr(mv[:], stats[:]))
                    own.wait()
                    nc.vector.tensor_scalar(var[:], mv[:, 1:2], LN_EPS, None, ALU.add).then_inc(var_ready, 1)
                    dve.wait_ge(std_ready, t + 1)
                    own.mark(nc.vector.reciprocal(rstd[:], std[:]))
                    own.wait()
                    nc.vector.tensor_scalar(xn_t[:, i, :], x1_t[:, i, :], mv[:, 0:1], rstd[:],
                                            ALU.subtract, ALU.mult).then_inc(normed, 1)

                def keep_logits(t):
                    dve.wait_ge(logits_done, t + 2)
                    nc.vector.tensor_copy(logits[:, bass.ds(t, 1), :].rearrange("p t e -> p (t e)"),
                                          logit_ps[:, 0:E]).then_inc(logits_read, 1)

                norm(0, 0, 0)
                with dve.Fori(0, LAST) as j:
                    norm(j * 2 + 1, 1, j)
                    keep_logits(j * 2)
                    norm(j * 2 + 2, 0, j + 1)
                    keep_logits(j * 2 + 1)
                norm(NT - 1, 1, LAST)
                keep_logits(NT - 2)
                keep_logits(NT - 1)

            @block.scalar
            def _(act):
                act.sem_inc(turned_copied, 2)

                def root(t):
                    act.wait_ge(var_ready, t + 1)
                    nc.scalar.activation(std[:], var[:], ACT.Sqrt).then_inc(std_ready, 1)

                def finish(t, i):
                    act.wait_ge(normed, t + 1)
                    nc.scalar.activation(sq[:, i, :], xn_t[:, i, :], ACT.Square,
                                         accum_out=squares[:, bass.ds(t, 1)])
                    for g in range(2):
                        act.wait_ge(turned, t * 2 + (g + 1))
                        act.wait_ge(logits_done, t + 1)
                        nc.scalar.copy(xnT[:, g * 4:g * 4 + 4, :], turn_ps[g][:]).then_inc(turned_copied, 1)

                root(0)
                with act.Fori(0, LAST) as j:
                    finish(j * 2, 0)
                    root(j * 2 + 1)
                    finish(j * 2 + 1, 1)
                    root(j * 2 + 2)
                finish(NT - 2, 0)
                root(NT - 1)
                finish(NT - 1, 1)


def route_stage(nc, a, gates, logits, squares, supers, slot_info):
    with ExitStack() as ctx:
        sb = lambda name, shape, dt=F32: ctx.enter_context(nc.sbuf_tensor(name, shape, dt))
        ps = lambda name, shape: ctx.enter_context(nc.psum_tensor(name, shape, F32))
        sem = lambda name: ctx.enter_context(nc.semaphore(name))
        W = [P, NT, E]
        scale = sb("expert_scale", [P, E])
        before = sb("before", [P, P])
        ones = sb("ones", [P, P])
        iota_e = sb("iota_e", [P, E])
        steps = sb("steps", [P, NT])
        sup_steps = sb("sup_steps", [P, 3])
        iota_s = sb("iota_s", [P, NSUP])
        info = sb("info", [P, 2, NT, 2])
        rms = sb("r_rms", [P, NT])
        root = sb("r_root", [P, NT])
        lg, low, prob = sb("lg", W), sb("low", W), sb("r_prob", W)
        tmp, coef, both = sb("r_tmp", W), sb("r_coef", W), sb("r_both", W)
        hot = [sb(f"hot{k}", W) for k in range(2)]
        pick = sb("pick", [P, NT])
        best = sb("best", [P, NT])
        norm = sb("r_norm", [P, NT])
        part = sb("r_part", [P, NT])
        rank, tot, pre = sb("rank", W), sb("tot", W), sb("pre", W)
        cnt, tiles, sups = sb("cnt", [P, E]), sb("tiles", [P, E]), sb("sups", [P, E])
        tile0, sup0, row0 = sb("tile0", [P, E]), sb("sup0", [P, E]), sb("row0", [P, E])
        over = sb("over", [P, E, NT])
        slot = sb("slot", [P, 2, NT], U32)
        SW = [1, NSUP, E]
        s_hot, s_rel, s_tmp = sb("s_hot", SW), sb("s_rel", SW), sb("s_tmp", SW)
        s_f = sb("s_f", [1, NSUP + 1, 4])
        rank_ps, tot_ps = ps("rank_ps", [P, 512]), ps("tot_ps", [P, 512])
        consts_in, own_sem = sem("r_consts_in"), sem("r_own")
        ms_ready, root_ready, diff_ready, exp_ready = sem("r_ms"), sem("r_root_ready"), sem("r_diff"), sem("r_exp")
        both_ready, ranked, info_ready, scattered = sem("r_both_ready"), sem("r_ranked"), sem("r_info"), sem("r_scattered")
        over_e = lambda t: t[:].unsqueeze(2).to_broadcast(W)
        over_t = lambda t: t[:].unsqueeze(1).to_broadcast(W)

        with nc.Block() as block:
            @block.sync
            def _(sp):
                for dst, src in ((scale, "expert_scale"), (before, "before"), (ones, "ones"), (iota_e, "iota_e"),
                                 (steps, "steps"), (sup_steps, "sup_steps"), (iota_s, "iota_s")):
                    sp.dma_start(dst[:], a[src]).then_inc(consts_in, 16)
                for k in range(2):
                    sp.dma_start(info[:, k, :, 0], a["token"], allow_slow_non_contiguous=True).then_inc(consts_in, 16)

            @block.scalar
            def _(act):
                act.wait_ge(ms_ready, 1)
                nc.scalar.activation(root[:], rms[:], ACT.Sqrt).then_inc(root_ready, 1)
                act.wait_ge(diff_ready, 1)
                nc.scalar.activation(prob[:], tmp[:], ACT.Exp).then_inc(exp_ready, 1)

            @block.tensor
            def _(pe):
                pe.wait_ge(consts_in, 16 * 9)
                pe.wait_ge(both_ready, 1)
                flat = both[:].rearrange("p t e -> p (t e)")
                nc.tensor.matmul(rank_ps[:, 0:NT * E], before[:], flat, start=True, stop=True)
                nc.tensor.matmul(tot_ps[:, 0:NT * E], ones[:], flat, start=True, stop=True).then_inc(ranked, 1)

            @block.gpsimd
            def _(pool):
                pool.wait_ge(info_ready, 1)
                for k in range(2):
                    for t in range(NT):
                        pool.indirect_dma_start(slot_info, bass.IndirectOffsetOnAxis(slot[:, k, t:t + 1], 0),
                                                info[:, k, t, :], None).then_inc(scattered, 16)
                pool.wait_ge(scattered, 16 * 2 * NT)

            @block.vector
            def _(dve):
                own = Count(dve, own_sem)

                def do(ins):
                    own.mark(ins)
                    own.wait()

                v = nc.vector
                v.tensor_scalar(rms[:], squares[:], 1.0 / D, RMS_EPS, ALU.mult, ALU.add).then_inc(ms_ready, 1)
                dve.wait_ge(root_ready, 1)
                do(v.reciprocal(rms[:], root[:]))
                do(v.tensor_scalar(rms[:], rms[:], float(D) ** -0.5, None, ALU.mult))
                do(v.tensor_tensor(lg[:], logits[:], over_e(rms), ALU.mult))
                dve.wait_ge(consts_in, 16 * 9)
                for k in range(2):
                    src = lg if k == 0 else low
                    do(v.tensor_reduce(best[:], src[:], AX_X, ALU.max))
                    if k == 0:
                        v.tensor_tensor(tmp[:], lg[:], over_e(best), ALU.subtract).then_inc(diff_ready, 1)
                    do(v.tensor_tensor(coef[:], src[:], over_e(best), ALU.is_lt))
                    do(v.scalar_tensor_tensor(coef[:], coef[:], 100.0, over_t(iota_e), ALU.mult, ALU.add))
                    do(v.tensor_reduce(pick[:], coef[:], AX_X, ALU.min))
                    do(v.tensor_tensor(hot[k][:], over_t(iota_e), over_e(pick), ALU.is_equal))
                    if k == 0:
                        do(v.scalar_tensor_tensor(low[:], hot[0][:], -1e30, lg[:], ALU.mult, ALU.add))
                v.tensor_tensor(both[:], hot[0][:], hot[1][:], ALU.add).then_inc(both_ready, 1)
                dve.wait_ge(both_ready, 1)
                dve.wait_ge(exp_ready, 1)
                do(v.tensor_reduce(norm[:], prob[:], AX_X, ALU.add))
                do(v.reciprocal(norm[:], norm[:]))
                do(v.tensor_tensor(prob[:], prob[:], over_e(norm), ALU.mult))
                do(v.tensor_tensor(tmp[:], prob[:], both[:], ALU.mult))
                do(v.tensor_reduce(norm[:], tmp[:], AX_X, ALU.add))
                do(v.scalar_tensor_tensor(norm[:], norm[:], 0.0, norm[:], ALU.is_le, ALU.add))
                do(v.reciprocal(norm[:], norm[:]))
                do(v.tensor_tensor(coef[:], prob[:], over_t(scale), ALU.mult))
                do(v.tensor_tensor(coef[:], coef[:], over_e(norm), ALU.mult))
                do(v.tensor_scalar(coef[:], coef[:], gates[:, 1:2], None, ALU.mult))
                dve.wait_ge(ranked, 1)
                do(v.tensor_copy(tot[:], tot_ps[:, 0:NT * E].rearrange("p (t e) -> p t e", e=E)))
                do(v.tensor_copy(rank[:], rank_ps[:, 0:NT * E].rearrange("p (t e) -> p t e", e=E)))
                do(v.memset(pre[:, 0, :], 0.0))
                for t in range(1, NT):
                    do(v.tensor_tensor(pre[:, t, :], pre[:, t - 1, :], tot[:, t - 1, :], ALU.add))
                do(v.tensor_tensor(cnt[:], pre[:, NT - 1, :], tot[:, NT - 1, :], ALU.add))
                do(v.tensor_tensor(over[:], cnt[:].unsqueeze(2).to_broadcast([P, E, NT]),
                                   steps[:].unsqueeze(1).to_broadcast([P, E, NT]), ALU.is_gt))
                do(v.tensor_reduce(tiles[:], over[:], AX_X, ALU.add))
                do(v.tensor_tensor(over[:, :, 0:3], tiles[:].unsqueeze(2).to_broadcast([P, E, 3]),
                                   sup_steps[:].unsqueeze(1).to_broadcast([P, E, 3]), ALU.is_gt))
                do(v.tensor_reduce(sups[:], over[:, :, 0:3], AX_X, ALU.add))
                for first, size in ((tile0, tiles), (sup0, sups)):
                    do(v.memset(first[:, 0:1], 0.0))
                    for e in range(1, E):
                        do(v.tensor_tensor(first[:, e:e + 1], first[:, e - 1:e], size[:, e - 1:e], ALU.add))
                do(v.tensor_scalar(row0[:], tile0[:], float(P), None, ALU.mult))
                do(v.tensor_tensor(rank[:], rank[:], pre[:], ALU.add))
                do(v.tensor_tensor(rank[:], rank[:], over_t(row0), ALU.add))
                for k in range(2):
                    do(v.tensor_tensor(tmp[:], hot[k][:], rank[:], ALU.mult))
                    do(v.tensor_reduce(part[:], tmp[:], AX_X, ALU.add))
                    do(v.tensor_copy(slot[:, k, :], part[:]))
                    do(v.tensor_tensor(tmp[:], hot[k][:], coef[:], ALU.mult))
                    do(v.tensor_reduce(info[:, k, :, 1], tmp[:], AX_X, ALU.add))
                v.memset(s_f[:], 0.0).then_inc(info_ready, 1)
                dve.wait_ge(info_ready, 1)
                se = lambda t: t[0:1, :].unsqueeze(1).to_broadcast(SW)
                ss = iota_s[0:1, :].unsqueeze(2).to_broadcast(SW)
                do(v.tensor_tensor(s_rel[:], ss, se(sup0), ALU.subtract))
                do(v.tensor_tensor(s_hot[:], s_rel[:], se(sups), ALU.is_lt))
                do(v.tensor_scalar(s_tmp[:], s_rel[:], 0.0, None, ALU.is_ge))
                do(v.tensor_tensor(s_hot[:], s_hot[:], s_tmp[:], ALU.mult))
                do(v.tensor_scalar(s_rel[:], s_rel[:], float(ST), None, ALU.mult))
                do(v.tensor_tensor(s_tmp[:], s_hot[:], se(iota_e), ALU.mult))
                do(v.tensor_reduce(s_f[:, 0:NSUP, 0], s_tmp[:], AX_X, ALU.add))
                do(v.tensor_tensor(s_tmp[:], se(tiles), s_rel[:], ALU.subtract))
                do(v.tensor_tensor(s_tmp[:], s_tmp[:], s_hot[:], ALU.mult))
                do(v.tensor_reduce(s_f[:, 0:NSUP, 1], s_tmp[:], AX_X, ALU.add))
                do(v.tensor_scalar(s_f[:, 0:NSUP, 1], s_f[:, 0:NSUP, 1], float(ST), None, ALU.min))
                do(v.tensor_tensor(s_tmp[:], se(tile0), s_rel[:], ALU.add))
                do(v.tensor_tensor(s_tmp[:], s_tmp[:], s_hot[:], ALU.mult))
                do(v.tensor_reduce(s_f[:, 0:NSUP, 2], s_tmp[:], AX_X, ALU.add))
                do(v.tensor_copy(s_f[:, 1:NSUP + 1, 3], s_f[:, 0:NSUP, 2]))
                do(v.tensor_copy(supers[:], s_f[:]))


def experts_stage(nc, a, ident, supers, slot_info, xn_rows, out):
    with ExitStack() as ctx:
        sb = lambda name, shape, dt=F32: ctx.enter_context(nc.sbuf_tensor(name, shape, dt))
        ps = lambda name, shape: ctx.enter_context(nc.psum_tensor(name, shape, F32))
        sem = lambda name: ctx.enter_context(nc.semaphore(name))
        NC_UP, NC = 4, 6
        HC = HID // NC_UP
        NR, HF = 3, FC // 2
        w_raw = [sb(f"w_raw{i}", [P, HF, 512]) for i in range(NR)]
        w_hi = [sb(f"w_hi{i}", [P, FC, 512], F32R) for i in range(2)]
        w_lo = [sb(f"w_lo{i}", [P, FC, 512], F32R) for i in range(2)]
        info = sb("e_info", [P, ST, 2])
        coef = sb("e_coef", [P, ST])
        token = sb("e_token", [P, ST], U32)
        place = sb("e_place", [P, 2, ST], U32)
        x_t = sb("e_x_t", [P, ST, D])
        xT_hi = sb("e_xT_hi", [P, ST, FC, P], F32R)
        xT_lo = sb("e_xT_lo", [P, ST, FC, P], F32R)
        hid = sb("e_hid", [P, ST, HC])
        hidT_hi = sb("e_hidT_hi", [P, ST, FC, P], F32R)
        hidT_lo = sb("e_hidT_lo", [P, ST, FC, P], F32R)
        y = sb("e_y", [P, 4, 512])
        spare = sb("e_spare", [P, 32])
        warm = sb("e_warm", [P, 1])
        unit_ps = [ps(f"unit_ps{i}", [P, 512]) for i in range(4)]
        turn_ps = [ps(f"e_turn_ps{i}", [P, 4, P]) for i in range(2)]
        hidT_ps = ps("hidT_ps", [P, 2, P])

        w_in = [sem(f"e_w_in{i}") for i in range(NR)]
        w_hi_done, w_lo_done = sem("e_w_hi_done"), sem("e_w_lo_done")
        xT_hi_done, hidT_hi_done = sem("e_xT_hi_done"), sem("e_hidT_hi_done")
        info_in, info_used = sem("e_info_in"), sem("e_info_used")
        x_in = [sem(f"e_x_in{t}") for t in range(ST)]
        turned, turned_copied = sem("e_turned"), sem("e_turned_copied")
        unit_done, unit_read = sem("e_unit_done"), sem("e_unit_read")
        gelu_ready = sem("e_gelu_ready")
        hidT_done, hidT_copied = sem("e_hidT_done"), sem("e_hidT_copied")
        y_added, y_free = sem("e_y_added"), sem("e_y_free")
        pool_own, spare_set, warmed = sem("e_pool_own"), sem("e_spare_set"), sem("e_warmed")
        spot = lambda c, t: 2 * (c % 2) + t % 2

        def read(eng, s, col, top):
            return eng.value_load(supers[0:1, bass.ds(s, 1), col:col + 1].rearrange("p s c -> p (s c)"), min_val=0, max_val=top)

        with nc.Block() as block:
            @block.sync
            def _(sp):
                def load_info(s):
                    sp.dma_start(info[:], slot_info[bass.ds(read(sp, s, 2, MAXT) * P, ST * P), :]
                                 .rearrange("(t p) c -> p t c", p=P)).then_inc(info_in, 16)

                load_info(0)
                with sp.Fori(0, NSUP) as s:
                    n = read(sp, s, 1, ST)
                    e = read(sp, s, 0, E - 1)
                    more = read(sp, s + 1, 1, ST)
                    with sp.If(n > 0):
                        for j in range(2 * NC):
                            c = j // 2
                            sp.wait_ge(w_lo_done, s * (2 * NC) + (j + 1))
                            src = a["gate_up"][e * NC_UP + c] if c < NC_UP else a["linear"][e * 2 + (c - NC_UP)]
                            sp.dma_start(w_raw[j % NR][:], src[:, (j % 2) * HF:(j % 2 + 1) * HF, :]).then_inc(w_in[j % NR], 16)
                        with sp.If(more > 0):
                            sp.wait_ge(info_used, s * 3 + 3)
                            load_info(s + 1)
                        sp.wait_ge(info_used, 3)

            @block.gpsimd
            def _(pool):
                pool.sem_inc(y_free, 2)

                places = iter(range(1, 32))

                def carry():
                    at = next(places)
                    return pool.tensor_tensor(spare[:, at:at + 1], spare[:, 0:1], spare[:, 0:1], ALU.add)

                def gather(s, base):
                    own = Count(pool, pool_own, base)
                    pool.wait_ge(info_in, s * 16 + 16)
                    carry()
                    own.mark(pool.tensor_copy(token[:], info[:, :, 0]))
                    own.wait()
                    carry()
                    for t in range(ST):
                        pool.indirect_dma_start(x_t[:, t, :], None, xn_rows,
                                                bass.IndirectOffsetOnAxis(token[:, t:t + 1], 0)).then_inc(x_in[t], 16)

                pool.memset(spare[:], 0.0).then_inc(spare_set, 1)
                pool.wait_ge(spare_set, 1)
                gather(0, 0)
                with pool.Fori(0, NSUP) as s:
                    n, first = read(pool, s, 1, ST), read(pool, s, 2, MAXT)
                    more = read(pool, s + 1, 1, ST)
                    with pool.If(n > 0):
                        pool.wait_ge(info_in, s * 16 + 16)
                        for t in range(ST):
                            pool.wait_ge(x_in[t], s * 16 + 16)
                        carry()
                        pool.tensor_scalar(place[:, 0, :], info[:, :, 0], 2.0, None, ALU.mult).then_inc(info_used, 1)
                        pool.tensor_scalar(place[:, 1, :], info[:, :, 0], 2.0, 1.0, ALU.mult, ALU.add).then_inc(info_used, 1)
                        pool.wait_ge(info_used, s * 3 + 3)
                        carry()
                        with pool.If(more > 0):
                            pool.wait_ge(turned, (first + n) * 2)
                            gather(s + 1, s + 1)
                        for c in range(2):
                            for t in range(ST):
                                unit = first * 2 + n * c + t
                                with pool.If(n > t):
                                    pool.wait_ge(unit_read, first * NC + n * (NC_UP + c) + (t + 3))
                                    carry()
                                    pool.indirect_dma_start(out, bass.IndirectOffsetOnAxis(place[:, c, t:t + 1], 0),
                                                            y[:, spot(c, t), :], None,
                                                            compute_op=ALU.add).then_inc(y_added, 16)
                                    pool.wait_ge(y_added, unit * 16 + 16)
                                    carry().then_inc(y_free, 1)
                                pool.wait_ge(spare_set, 1)

            @block.tensor
            def _(pe):
                pe.sem_inc(unit_done, 1)
                with pe.Fori(0, NSUP) as s:
                    n, first = read(pe, s, 1, ST), read(pe, s, 2, MAXT)

                    def turn(t):
                        pe.wait_ge(x_in[t], s * 16 + 16)
                        for g in range(2):
                            pe.wait_ge(turned_copied, first * 2 + (2 * t + g + 1))
                            for f in range(4):
                                k = g * 4 + f
                                mm = nc.tensor.transpose(turn_ps[g][:, f, :], x_t[:, t, k * P:(k + 1) * P], ident[:])
                            mm.then_inc(turned, 1)

                    def unit(c, t):
                        if t == 0:
                            pe.wait_ge(w_lo_done, s * (2 * NC) + (2 * c + 2 + NR))
                        if c == 0:
                            pe.wait_ge(turned_copied, (first + t) * 2 + 4)
                        if c == NC_UP:
                            pe.wait_ge(hidT_copied, first * 4 + n * 3 + (t + 2))
                        pe.wait_ge(unit_read, first * NC + n * c + (t + 1))
                        left_hi, left_lo = (xT_hi, xT_lo) if c < NC_UP else (hidT_hi, hidT_lo)
                        for k in range(FC):
                            mm = split_product(nc, unit_ps[spot(c, t)][:], (left_hi[:, t, k, :], left_lo[:, t, k, :]),
                                               (w_hi[c % 2][:, k, :], w_lo[c % 2][:, k, :]), k == 0, k == FC - 1)
                        mm.then_inc(unit_done, 1)

                    def turn_hidden(c, t):
                        pe.wait_ge(unit_read, first * NC + n * c + (t + 3))
                        pe.wait_ge(hidT_copied, first * 4 + n * c + (t + 1))
                        for k in range(2):
                            mm = nc.tensor.transpose(hidT_ps[:, k, :], hid[:, t, k * P:(k + 1) * P], ident[:])
                        mm.then_inc(hidT_done, 1)

                    with pe.If(n > 0):
                        turn(0)
                        for t in range(ST):
                            if t + 1 < ST:
                                with pe.If(n > t + 1):
                                    turn(t + 1)
                                pe.wait_ge(x_in[0], 16)
                            with pe.If(n > t):
                                unit(0, t)
                            pe.wait_ge(x_in[0], 16)
                        for c in range(1, NC_UP):
                            for t in range(ST):
                                with pe.If(n > t):
                                    turn_hidden(c - 1, t)
                                    unit(c, t)
                                pe.wait_ge(x_in[0], 16)
                        turn_hidden(NC_UP - 1, 0)
                        for t in range(ST):
                            if t + 1 < ST:
                                with pe.If(n > t + 1):
                                    turn_hidden(NC_UP - 1, t + 1)
                                pe.wait_ge(x_in[0], 16)
                            with pe.If(n > t):
                                unit(NC_UP, t)
                            pe.wait_ge(x_in[0], 16)
                        for t in range(ST):
                            with pe.If(n > t):
                                unit(NC_UP + 1, t)
                            pe.wait_ge(x_in[0], 16)

            @block.scalar
            def _(act):

                def split_high(s, c, free):
                    for h in range(2):
                        j = 2 * c + h
                        act.wait_ge(w_in[j % NR], s * (16 * 2 * NC // NR) + 16 * (j // NR + 1))
                        if h == 0:
                            act.wait_ge(unit_done, free)
                        nc.scalar.copy(w_hi[c % 2][:, h * HF:(h + 1) * HF, :], w_raw[j % NR][:]).then_inc(w_hi_done, 1)

                nc.scalar.activation(warm[:], ident[:, 0:1], ACT.Gelu_apprx_tanh).then_inc(warmed, 1)
                split_high(0, 0, 1)
                with act.Fori(0, NSUP) as s:
                    n, first = read(act, s, 1, ST), read(act, s, 2, MAXT)
                    more = read(act, s + 1, 1, ST)

                    def gate(c, t):
                        act.wait_ge(unit_done, first * NC + n * c + (t + 2))
                        nc.scalar.activation(hid[:, t, :], unit_ps[spot(c, t)][:, 0:HC],
                                             ACT.Gelu_apprx_tanh).then_inc(gelu_ready, 1)

                    def keep(c, t):
                        act.wait_ge(hidT_done, first * 4 + n * c + (t + 1))
                        nc.scalar.copy(hidT_hi[:, t, 2 * c:2 * c + 2, :], hidT_ps[:]).then_inc(hidT_hi_done, 1)

                    with act.If(n > 0):
                        for c in range(NC_UP + 1):
                            for t in range(ST):
                                with act.If(n > t):
                                    if c:
                                        keep(c - 1, t)
                                    if c < NC_UP:
                                        gate(c, t)
                                act.wait_ge(unit_done, 1)
                                if t == 0:
                                    split_high(s, c + 1, first * NC + n * c + 1)
                        with act.If(more > 0):
                            split_high(s + 1, 0, first * NC + n * (NC - 1) + 1)
                        act.wait_ge(unit_done, 1)

            @block.vector
            def _(dve):
                dve.sem_inc(turned_copied, 2)
                dve.sem_inc(unit_read, 2)
                dve.sem_inc(hidT_copied, 1)
                dve.sem_inc(w_lo_done, NR)

                def split_low(s, c):
                    for h in range(2):
                        j = 2 * c + h
                        dve.wait_ge(w_hi_done, s * (2 * NC) + (j + 1))
                        nc.vector.tensor_tensor(w_lo[c % 2][:, h * HF:(h + 1) * HF, :], w_raw[j % NR][:],
                                                w_hi[c % 2][:, h * HF:(h + 1) * HF, :], ALU.subtract).then_inc(w_lo_done, 1)

                split_low(0, 0)
                with dve.Fori(0, NSUP) as s:
                    n, first = read(dve, s, 1, ST), read(dve, s, 2, MAXT)
                    more = read(dve, s + 1, 1, ST)

                    def keep_x(t):
                        for g in range(2):
                            dve.wait_ge(turned, first * 2 + (2 * t + g + 1))
                            nc.vector.tensor_copy(xT_hi[:, t, 4 * g:4 * g + 4, :], turn_ps[g][:]).then_inc(xT_hi_done, 1)
                            dve.wait_ge(xT_hi_done, first * 2 + (2 * t + g + 1))
                            nc.vector.tensor_tensor(xT_lo[:, t, 4 * g:4 * g + 4, :], turn_ps[g][:],
                                                    xT_hi[:, t, 4 * g:4 * g + 4, :], ALU.subtract).then_inc(turned_copied, 1)

                    def keep_hidden(c, t):
                        dve.wait_ge(hidT_hi_done, first * 4 + n * c + (t + 1))
                        nc.vector.tensor_tensor(hidT_lo[:, t, 2 * c:2 * c + 2, :], hidT_ps[:],
                                                hidT_hi[:, t, 2 * c:2 * c + 2, :], ALU.subtract).then_inc(hidT_copied, 1)

                    def times_up(c, t):
                        dve.wait_ge(gelu_ready, first * 4 + n * c + (t + 1))
                        nc.vector.tensor_tensor(hid[:, t, :], hid[:, t, :], unit_ps[spot(c, t)][:, HC:2 * HC],
                                                ALU.mult).then_inc(unit_read, 1)

                    def weigh(c, t):
                        unit = first * 2 + n * c + t
                        dve.wait_ge(unit_done, first * NC + n * (NC_UP + c) + (t + 2))
                        dve.wait_ge(y_free, unit + 1)
                        nc.vector.tensor_scalar(y[:, spot(c, t), :], unit_ps[spot(NC_UP + c, t)][:], coef[:, t:t + 1], None,
                                                ALU.mult).then_inc(unit_read, 1)

                    with dve.If(n > 0):
                        dve.wait_ge(info_in, s * 16 + 16)
                        dve.wait_ge(unit_read, first * NC + 2)
                        nc.vector.tensor_copy(coef[:], info[:, :, 1]).then_inc(info_used, 1)
                        keep_x(0)
                        for t in range(ST):
                            if t + 1 < ST:
                                with dve.If(n > t + 1):
                                    keep_x(t + 1)
                                dve.wait_ge(info_in, 16)
                            with dve.If(n > t):
                                times_up(0, t)
                            dve.wait_ge(info_in, 16)
                            if t == 0:
                                split_low(s, 1)
                        for c in range(1, NC_UP):
                            for t in range(ST):
                                with dve.If(n > t):
                                    keep_hidden(c - 1, t)
                                    times_up(c, t)
                                dve.wait_ge(info_in, 16)
                                if t == 0:
                                    split_low(s, c + 1)
                        keep_hidden(NC_UP - 1, 0)
                        for t in range(ST):
                            if t + 1 < ST:
                                with dve.If(n > t + 1):
                                    keep_hidden(NC_UP - 1, t + 1)
                                dve.wait_ge(info_in, 16)
                            with dve.If(n > t):
                                weigh(0, t)
                            dve.wait_ge(info_in, 16)
                            if t == 0:
                                split_low(s, NC - 1)
                        for t in range(ST):
                            with dve.If(n > t):
                                weigh(1, t)
                            dve.wait_ge(info_in, 16)
                            if t == 0:
                                with dve.If(more > 0):
                                    split_low(s + 1, 0)
                                dve.wait_ge(info_in, 16)


def layout(x, ctx_2048, itok_BxS_0_1023, g_xattn, g_ffn, L0_xattn_W_kvc, L0_xattn_W_dq, L0_xattn_W_uq, L0_xattn_W_qr,
           L0_xattn_W_uk, L0_xattn_W_kr, L0_xattn_W_uv, L0_xattn_W_o, L0_ffn_router_logits, L0_ffn_gating_einsum,
           L0_ffn_linear, L0_ffn_per_expert_scale, L0_ffn_router_scale):
    n = lambda v: np.asarray(v)
    c = np.ascontiguousarray
    f32 = np.float32
    rows = lambda w: c(n(w).reshape(-1, P, w.shape[-1]).transpose(1, 0, 2))
    half = R // 2
    freq = (1.0 / 10000.0 ** (np.arange(half, dtype=f32) / f32(half))).astype(f32)
    angle = lambda m: np.arange(m, dtype=f32)[:, None] * freq
    seg = n(itok_BxS_0_1023).reshape(NTOK)

    r = np.arange(P) % SL
    is_mean = r == SL - 1
    q_of = np.where(is_mean, 0, (np.arange(P) // SL) * QS + r // WIN)
    groups = np.arange(GROUPS)
    window = c(seg.reshape(GROUPS, GQ)[:, q_of].T)
    back = np.where(is_mean, 0, r % WIN - BACK).astype(f32)[:, None]
    keep = np.where(is_mean, 0.0, 1.0).astype(f32)[:, None]
    batch_of = groups // NG
    base = np.where(is_mean[:, None], BATCH * LK + batch_of, LK * batch_of).astype(f32)

    row_q = np.arange(RW) // H
    col = np.arange(SL)
    mean_col = col == SL - 1
    own = (row_q[:, None] == (col // WIN)[None]) & ~mean_col
    mid = (LK - 1) / 2
    span = (LK - 1 + BACK) / 2
    big = 1e30
    ma = np.where(own, (col % WIN - BACK)[None] - mid, np.where(mean_col[None], -span, 0.0)).astype(f32)
    mb = np.where(own, -big, np.where(mean_col[None], big, 0.0)).astype(f32) + np.zeros((RW, 1), f32)
    mc = np.where(own, big * (mid + 0.5) ** 2, np.where(mean_col[None], -big * (span + 0.5) ** 2, -big)).astype(f32)
    ks, qs = angle(LK), angle(LQ)
    both = lambda t: np.concatenate([t, t], axis=1)
    gw = n(L0_ffn_gating_einsum).reshape(E, 2, 4, HID // 4, FC, P)
    lw = n(L0_ffn_linear).reshape(E, FC, P, 2, F // 2)
    wk = n(L0_xattn_W_kvc)
    fill = np.zeros((SLOTS, 2), f32)
    fill[:, 0] = NTOK + np.arange(SLOTS) % P
    return dict(
        x=n(x).reshape(NT, P, D),
        ctxT=c(n(ctx_2048).reshape(BATCH, KT, KN, FC, P).transpose(0, 1, 4, 3, 2)).reshape(BATCH * KT, P, FC, KN),
        w_kvc=rows(wk), w_kvcT=rows(c(wk.T)), w_kr=rows(L0_xattn_W_kr), w_dq=rows(L0_xattn_W_dq),
        w_uq=rows(L0_xattn_W_uq), w_qr=rows(L0_xattn_W_qr),
        w_ukT=c(n(L0_xattn_W_uk).reshape(KVC, H, HD).transpose(2, 1, 0)),
        w_uv=rows(L0_xattn_W_uv), w_o=rows(L0_xattn_W_o),
        window=window, seg_rows=c(np.repeat(seg.reshape(2 * GROUPS, QS).T, H, axis=0)),
        back=back, keep=keep, base=c(base), ma=ma, mb=mb, mc=mc,
        kcos=c(both(np.cos(ks)).astype(f32).reshape(KT, KN, R).transpose(1, 0, 2)),
        ksin=c(both(np.sin(ks)).astype(f32).reshape(KT, KN, R).transpose(1, 0, 2)),
        qcos=c(np.tile(np.cos(qs), (1, 4)).astype(f32).T),
        qsin=c(np.tile(np.concatenate([np.sin(qs), -np.sin(qs)], axis=1), (1, 2)).astype(f32).T),
        ident=np.eye(P, dtype=f32), inv=np.full((KN, 1), 1.0 / LK, f32),
        gates=np.repeat(np.concatenate([n(g_xattn), n(g_ffn)])[None], P, axis=0),
        router=rows(L0_ffn_router_logits), router_scale=c(n(L0_ffn_router_scale).reshape(FC, P).T),
        expert_scale=np.repeat(n(L0_ffn_per_expert_scale)[None], P, axis=0),
        before=np.triu(np.ones((P, P), f32), 1), ones=np.ones((P, P), f32),
        token=c(np.arange(NTOK, dtype=f32).reshape(NT, P).T),
        gate_up=c(gw.transpose(0, 2, 5, 4, 1, 3)).reshape(E * 4, P, FC, 2 * HID // 4),
        linear=c(lw.transpose(0, 3, 2, 1, 4)).reshape(E * 2, P, FC, F // 2),
        slot_fill=fill, iota_e=np.repeat(np.arange(E, dtype=f32)[None], P, axis=0),
        steps=np.repeat(P * np.arange(NT, dtype=f32)[None], P, axis=0),
        sup_steps=np.repeat(ST * np.arange(3, dtype=f32)[None], P, axis=0),
        iota_s=np.repeat(np.arange(NSUP, dtype=f32)[None], P, axis=0),
    )


def kernel(**inputs):
    import numpy as _np
    import concourse.bacc as _bacc
    from concourse import mybir as _mybir
    from concourse.bass_utils import run_bass_kernel_spmd as _run

    arrays = {f"in_{k}": _np.ascontiguousarray(v) for k, v in layout(**inputs).items()}
    nc = _bacc.Bacc("TRN2", target_bir_lowering=False, num_devices=1)
    a = {k[3:]: nc.dram_tensor(k, v.shape, _mybir.dt.from_np(v.dtype), kind="ExternalInput").ap() for k, v in arrays.items()}
    out = nc.dram_tensor("out", (2 * (NTOK + P), D // 2), F32, kind="ExternalOutput").ap()
    program(nc, a, out)
    r = _run(nc, [arrays], core_ids=[0])
    return r.results[0]["out"][:2 * NTOK].reshape(BATCH, LQ, D)
```

```python
from contextlib import ExitStack

import numpy as np
import concourse.bass as bass
from concourse import mybir

F32 = mybir.dt.float32
F32R = mybir.dt.float32r
I32 = mybir.dt.int32
U32 = mybir.dt.uint32
ALU = mybir.AluOpType
ACT = mybir.ActivationFunctionType
AX_X = mybir.AxisListType.X

P = 128
BATCH, LQ, D = 8, 224, 1024
LK = 750
NTOK = BATCH * LQ
NT = NTOK // P
FC = D // P
KVC, QC, R = 256, 384, 64
KW = KVC + R
H, HD = 16, 128
KT, KN = 6, LK // 6
QB = 448
BACK = 8
WIN = BACK + 1
QS = 7
GQ = 2 * QS
NG = LQ // GQ
GROUPS = BATCH * NG
RW = QS * H
SL = QS * WIN + 1
E, F, HID = 8, 1024, 1024
ST = 5
MAXT = 2 * NT + E - 1
NSUP = 2 * NTOK // (ST * P) + E
SLOTS = (MAXT + ST) * P
LN_EPS, RMS_EPS = 1e-5, 1e-6
SCALE = float(1.0 / np.sqrt(HD + R).astype(np.float32))
assert KN * KT == LK and SL * 2 == P and NG * GQ == LQ


def split_product(nc, out, left, right, start, stop):
    nc.tensor.matmul(out, left[0], right[0], start=start, stop=False)
    nc.tensor.matmul(out, left[0], right[1], start=False, stop=False)
    return nc.tensor.matmul(out, left[1], right[0], start=False, stop=stop)


class Count:

    def __init__(self, eng, sem, base=0):
        self.eng, self.sem, self.base, self.n = eng, sem, base, 0

    def mark(self, ins):
        ins.then_inc(self.sem, 1)
        self.n += 1

    def wait(self):
        self.eng.wait_ge(self.sem, self.base + self.n)


def program(nc, a, out, stop=9):
    with ExitStack() as whole:
        kv_rows = nc.dram_tensor("kv_rows", (BATCH * LK + BATCH, KW), F32).ap()
        qc_dram = nc.dram_tensor("qc_dram", (P, 3, NTOK), F32).ap()
        o_dram = nc.dram_tensor("o_dram", (P, H, NTOK), F32).ap()
        xn_rows = nc.dram_tensor("xn_rows", (NTOK + P, D), F32).ap()
        slot_info = nc.dram_tensor("slot_info", (SLOTS, 2), F32).ap()
        ident = whole.enter_context(nc.sbuf_tensor("ident", [P, P], F32))
        logits = whole.enter_context(nc.sbuf_tensor("logits", [P, NT, E], F32))
        gates = whole.enter_context(nc.sbuf_tensor("gates", [P, 2], F32))
        supers = whole.enter_context(nc.sbuf_tensor("supers", [1, NSUP + 1, 4], I32))
        squares = whole.enter_context(nc.sbuf_tensor("squares", [P, NT], F32))
        with ExitStack() as early:
            ahead = [early.enter_context(nc.sbuf_tensor(name, shape, F32)) for name, shape in
                     (("w_uq", [P, 3, H * HD]), ("w_qr", [P, 3, H * R]), ("w_ukT", [P, H, KVC]), ("w_uv", [P, 2, H * HD]))]
            ahead_in = early.enter_context(nc.semaphore("ahead_in"))
            keys_stage(nc, a, ident, gates, kv_rows, xn_rows, slot_info, ahead, ahead_in)
            if stop > 1:
                queries_stage(nc, a, ident, qc_dram)
            if stop > 2:
                attend_stage(nc, a, ident, ahead, ahead_in, kv_rows, qc_dram, o_dram)
        if stop > 3:
            project_stage(nc, a, ident, gates, logits, squares, o_dram, xn_rows, out)
        if stop > 4:
            route_stage(nc, a, gates, logits, squares, supers, slot_info)
        if stop > 5:
            experts_stage(nc, a, ident, supers, slot_info, xn_rows, out)


def keys_stage(nc, a, ident, gates, kv_rows, xn_rows, slot_info, ahead, ahead_in):
    with ExitStack() as ctx:
        sb = lambda name, shape, dt=F32: ctx.enter_context(nc.sbuf_tensor(name, shape, dt))
        ps = lambda name, shape: ctx.enter_context(nc.psum_tensor(name, shape, F32))
        sem = lambda name: ctx.enter_context(nc.semaphore(name))
        NBUF = 3
        ctx_t = sb("ctx_t", [P, NBUF, FC, KN])
        ctx_hi = sb("ctx_hi", [P, NBUF, FC, KN], F32R)
        ctx_lo = sb("ctx_lo", [P, NBUF, FC, KN], F32R)
        w_kv = sb("w_kv", [P, FC, KW])
        w_kv_hi = sb("w_kv_hi", [P, FC, KW], F32R)
        w_kv_lo = sb("w_kv_lo", [P, FC, KW], F32R)
        w_kvT = sb("w_kvT", [P, 2, D])
        w_kr = sb("w_kr", [P, 2, R])
        kcos = sb("kcos", [KN, KT, R])
        ksin = sb("ksin", [KN, KT, R])
        xcos = sb("xcos", [KN, 2, R])
        xsin = sb("xsin", [KN, 2, R])
        inv = sb("inv", [KN, 1])
        rows = sb("rows", [KN, 2, KW])
        means = sb("means", [P, 2, BATCH])
        mean_rows = sb("mean_rows", [2 * BATCH, P])
        zeros = sb("zeros", [P, D])
        fold_ps = ps("fold_ps", [P, 512])
        kv_ps = [ps(f"kv_ps{i}", [P, 512]) for i in range(2)]
        mean_ps = [ps(f"mean_ps{i}", [P, 512]) for i in range(2)]
        meanT_ps = ps("meanT_ps", [P, 512])

        weights_in = sem("k_weights_in")
        ctx_in = [sem(f"k_ctx_in{i}") for i in range(NBUF)]
        hi_done, lo_done = sem("k_hi_done"), sem("k_lo_done")
        fold_done = sem("k_fold_done")
        fold_copied = sem("k_fold_copied")
        w_own, w_split = sem("k_w_own"), sem("k_w_split")
        kv_done = sem("k_kv_done")
        kv_read = sem("k_kv_read")
        rows_ready = sem("k_rows_ready")
        rows_out = [sem(f"k_rows_out{i}") for i in range(2)]
        means_done = sem("k_means_done")
        mean_copied = sem("k_mean_copied")
        meanT_done = sem("k_meanT_done")
        meanT_copied = sem("k_meanT_copied")
        zeroed = sem("k_zeroed")
        fill_out = sem("k_fill_out")
        dve_own = sem("k_dve_own")
        gate_own = sem("k_gate_own")

        with nc.Block() as block:
            @block.sync
            def _(sp):
                for dst, src in ((w_kv[:, :, 0:KVC], a["w_kvc"]), (w_kvT[:], a["w_kvcT"]), (w_kr[:], a["w_kr"]),
                                 (kcos[:], a["kcos"]), (ksin[:], a["ksin"]), (ident[:], a["ident"]),
                                 (inv[:], a["inv"]), (gates[:], a["gates"])):
                    sp.dma_start(dst, src).then_inc(weights_in, 16)
                for t in range(NBUF):
                    sp.dma_start(ctx_t[:, t], a["ctxT"][t]).then_inc(ctx_in[t], 16)

                for i in range(2):
                    sp.sem_inc(rows_out[i], 16)
                w_uq, w_qr, w_ukT, w_uv = ahead
                with sp.Fori(0, BATCH) as b:
                    for w, name, share in ((w_uq, "w_uq", H * HD // BATCH), (w_qr, "w_qr", H * R // BATCH),
                                           (w_uv, "w_uv", H * HD // BATCH)):
                        cut = bass.ds(b * share, share)
                        sp.dma_start(w[:, :, cut], a[name][:, :, cut]).then_inc(ahead_in, 16)
                    cut = bass.ds(b * (H // BATCH), H // BATCH)
                    sp.dma_start(w_ukT[:, cut, :], a["w_ukT"][:, cut, :]).then_inc(ahead_in, 16)
                    for j in range(KT):
                        sp.wait_ge(rows_ready, b * KT + (j + 1))
                        sp.dma_start(kv_rows[bass.ds(b * LK + j * KN, KN), :], rows[:, j % 2, :]).then_inc(rows_out[j % 2], 16)
                sp.wait_ge(zeroed, 1)
                sp.dma_start(kv_rows[BATCH * LK:, KVC:], zeros[0:BATCH, 0:R]).then_inc(fill_out, 16)
                sp.dma_start(xn_rows[NTOK:, :], zeros[:]).then_inc(fill_out, 16)
                sp.dma_start(slot_info.rearrange("(t p) c -> p t c", p=P),
                             a["slot_fill"].rearrange("(t p) c -> p t c", p=P)).then_inc(fill_out, 16)
                sp.wait_ge(meanT_copied, 1)
                for k in range(2):
                    sp.dma_start(kv_rows[BATCH * LK:, k * P:(k + 1) * P],
                                 mean_rows[k * BATCH:(k + 1) * BATCH, :]).then_inc(fill_out, 16)
                sp.wait_ge(fill_out, 16 * 5)
                for i in range(2):
                    sp.wait_ge(rows_out[i], 16 * (BATCH * KT // 2 + 1))

            @block.gpsimd
            def _(pool):
                pool.memset(zeros[:], 0.0).then_inc(zeroed, 1)

            @block.tensor
            def _(pe):
                pe.sem_inc(means_done, 1)
                pe.sem_inc(kv_done, NBUF)
                pe.wait_ge(weights_in, 16 * 8)
                for f in range(FC):
                    for k in range(2):
                        mm = nc.tensor.matmul(fold_ps[:, f * R:(f + 1) * R], w_kvT[:, k, f * P:(f + 1) * P],
                                              w_kr[:, k, :], start=(k == 0), stop=(k == 1))
                mm.then_inc(fold_done, 1)
                pe.wait_ge(w_split, 1)

                def mean_part(b, j):
                    pe.wait_ge(rows_ready, b * KT + (j + 1))
                    if j == 0:
                        pe.wait_ge(mean_copied, b + 1)
                    for k in range(2):
                        mm = nc.tensor.matmul(mean_ps[k][:, 0:1], rows[:, j % 2, k * P:(k + 1) * P], inv[:],
                                              start=(j == 0), stop=(j == KT - 1))
                    mm.then_inc(means_done, 1)

                with pe.Fori(0, BATCH) as b:
                    for j in range(KT):
                        pe.wait_ge(lo_done, b * KT + (j + 1))
                        pe.wait_ge(kv_read, b * KT + max(j, 1))
                        for f in range(FC):
                            mm = split_product(nc, kv_ps[j % 2][0:KN, 0:KW],
                                               (ctx_hi[:, j % NBUF, f, :], ctx_lo[:, j % NBUF, f, :]),
                                               (w_kv_hi[:, f, :], w_kv_lo[:, f, :]), f == 0, f == FC - 1)
                        mm.then_inc(kv_done, 1)
                        if j:
                            mean_part(b, j - 1)
                    mean_part(b, KT - 1)
                pe.wait_ge(mean_copied, BATCH + 1)
                nc.tensor.transpose(meanT_ps[0:2 * BATCH, 0:P], means[:].rearrange("p k b -> p (k b)"),
                                    ident[:]).then_inc(meanT_done, 1)

            @block.vector
            def _(dve):
                dve.sem_inc(kv_read, 1)
                dve.sem_inc(mean_copied, 1)
                dve.wait_ge(fold_done, 1)
                nc.vector.tensor_copy(w_kv[:, :, KVC:KW],
                                      fold_ps[:].rearrange("p (f r) -> p f r", f=FC)).then_inc(fold_copied, 1)
                dve.wait_ge(fold_copied, 1)
                nc.vector.tensor_copy(w_kv_hi[:], w_kv[:]).then_inc(w_own, 1)
                dve.wait_ge(w_own, 1)
                nc.vector.tensor_tensor(w_kv_lo[:], w_kv[:], w_kv_hi[:], ALU.subtract).then_inc(w_split, 1)

                def split_low(t, slot):
                    dve.wait_ge(hi_done, t + 1)
                    nc.vector.tensor_tensor(ctx_lo[:, slot], ctx_t[:, slot], ctx_hi[:, slot], ALU.subtract).then_inc(lo_done, 1)

                def batch(b, last):
                    own = Count(dve, dve_own, b * (KT * 2))
                    for j in range(KT):
                        if not (last and j == KT - 1):
                            split_low(b * KT + (j + 1), (j + 1) % NBUF)
                        dve.wait_ge(kv_done, b * KT + (j + 1 + NBUF))
                        dve.wait_ge(rows_out[j % 2], b * (16 * KT // 2) + 16 * (j // 2 + 1))
                        dve.wait_ge(means_done, b * KT + max(j, 1))
                        pr = kv_ps[j % 2][0:KN, KVC:KW]
                        own.mark(nc.vector.tensor_tensor(xcos[:, j % 2, :], pr, kcos[:, j, :], ALU.mult))
                        own.mark(nc.vector.tensor_tensor(xsin[:, j % 2, :], pr, ksin[:, j, :], ALU.mult))
                        nc.vector.tensor_copy(rows[:, j % 2, 0:KVC], kv_ps[j % 2][0:KN, 0:KVC]).then_inc(kv_read, 1)
                        own.wait()
                        half = R // 2
                        nc.vector.tensor_tensor(rows[:, j % 2, KVC:KVC + half], xcos[:, j % 2, 0:half],
                                                xsin[:, j % 2, half:R], ALU.subtract)
                        nc.vector.tensor_tensor(rows[:, j % 2, KVC + half:KW], xsin[:, j % 2, 0:half],
                                                xcos[:, j % 2, half:R], ALU.add).then_inc(rows_ready, 1)
                    dve.wait_ge(means_done, b * KT + (KT + 1))
                    for k in range(2):
                        cp = nc.vector.tensor_copy(means[:, k, bass.ds(b, 1)], mean_ps[k][:, 0:1])
                    cp.then_inc(mean_copied, 1)

                split_low(0, 0)
                with dve.Fori(0, BATCH - 1) as b:
                    batch(b, False)
                batch(BATCH - 1, True)
                dve.wait_ge(meanT_done, 1)
                nc.vector.tensor_copy(mean_rows[:], meanT_ps[0:2 * BATCH, 0:P]).then_inc(meanT_copied, 1)

            @block.scalar
            def _(act):
                act.wait_ge(weights_in, 16 * 8)
                nc.scalar.activation(gates[:], gates[:], ACT.Tanh).then_inc(gate_own, 1)

                def batch(b, loads):
                    for j in range(KT):
                        act.wait_ge(ctx_in[j % NBUF], b * (16 * KT // NBUF) + 16 * (j // NBUF + 1))
                        act.wait_ge(kv_done, b * KT + (j + 1))
                        nc.scalar.copy(ctx_hi[:, j % NBUF], ctx_t[:, j % NBUF]).then_inc(hi_done, 1)
                        if j < loads:
                            act.wait_ge(lo_done, b * KT + (j + 1))
                            act.dma_start(ctx_t[:, j % NBUF], a["ctxT"][b * KT + (j + NBUF)]).then_inc(ctx_in[j % NBUF], 16)

                with act.Fori(0, BATCH - 1) as b:
                    batch(b, KT)
                batch(BATCH - 1, KT - NBUF)


def queries_stage(nc, a, ident, qc_dram):
    with ExitStack() as ctx:
        sb = lambda name, shape, dt=F32: ctx.enter_context(nc.sbuf_tensor(name, shape, dt))
        ps = lambda name, shape: ctx.enter_context(nc.psum_tensor(name, shape, F32))
        sem = lambda name: ctx.enter_context(nc.semaphore(name))
        w_dq = sb("w_dq", [P, FC, QC])
        NX = 4
        x_t = sb("x_t", [P, NX, D])
        xn_t = sb("xn_t", [P, 2, D])
        xnT = sb("xnT", [P, FC, NTOK])
        stats = sb("stats", [P, 2, 2, 6])
        mv = sb("mv", [P, 2, 2])
        rstd = sb("rstd", [P, 2])
        var = sb("var", [P, 2])
        spare = sb("spare", [P, 1])
        std = sb("std", [P, 2])
        qc_t = sb("qc_t", [P, 2, 3, QB])
        turn_ps = [ps(f"q_turn_ps{i}", [P, 4, P]) for i in range(2)]
        qc_ps = [ps(f"q_qc_ps{i}", [P, 512]) for i in range(3)]

        w_in = sem("q_w_in")
        x_in = [sem(f"q_x_in{i}") for i in range(NX)]
        var_ready = sem("q_var_ready")
        std_ready = sem("q_std_ready")
        normed = sem("q_normed")
        turned = sem("q_turned")
        turned_copied = sem("q_turned_copied")
        qc_done = sem("q_qc_done")
        qc_copied = sem("q_qc_copied")
        qc_out = [sem(f"q_qc_out{i}") for i in range(2)]
        dve_own = sem("q_dve_own")

        with nc.Block() as block:
            @block.sync
            def _(sp):
                for i in range(NX):
                    sp.dma_start(x_t[:, i], a["x"][i]).then_inc(x_in[i], 16)
                sp.dma_start(w_dq[:], a["w_dq"]).then_inc(w_in, 16)

                def reload(t, slot):
                    sp.wait_ge(normed, t + 1)
                    sp.dma_start(x_t[:, slot], a["x"][t + NX]).then_inc(x_in[slot], 16)

                with sp.Fori(0, NT // NX - 1) as m:
                    for i in range(NX):
                        reload(m * NX + i, i)
                for i in range(NT % NX):
                    reload((NT // NX - 1) * NX + i, i)
                for i in range(2):
                    sp.sem_inc(qc_out[i], 16)
                with sp.Fori(0, NTOK // QB // 2) as n2:
                    for i in range(2):
                        sp.wait_ge(qc_copied, n2 * 6 + (3 * (i + 1) + 1))
                        sp.dma_start(qc_dram[:, :, bass.ds(n2 * (2 * QB) + i * QB, QB)], qc_t[:, i]).then_inc(qc_out[i], 16)
                for i in range(2):
                    sp.wait_ge(qc_out[i], 16 * (NTOK // QB // 2 + 1))

            @block.vector
            def _(dve):
                dve.sem_inc(qc_copied, 1)

                def pair(t, m, slot):
                    own = Count(dve, dve_own, t * 4)
                    for i in range(2):
                        dve.wait_ge(x_in[slot + i], m * 16 + 16)
                        for h in range(2):
                            own.mark(nc.vector.bn_stats(stats[:, i, h, :], x_t[:, slot + i, h * 512:(h + 1) * 512]))
                        own.wait()
                        nc.vector.tensor_copy(spare[:], stats[:, i, 0, 0:1])
                        own.mark(nc.vector.bn_aggr(mv[:, i, :], stats[:, i]))
                        own.wait()
                        nc.vector.tensor_scalar(var[:, i:i + 1], mv[:, i, 1:2], LN_EPS, None, ALU.add).then_inc(var_ready, 1)
                    for i in range(2):
                        dve.wait_ge(std_ready, t + (i + 1))
                        own.mark(nc.vector.reciprocal(rstd[:, i:i + 1], std[:, i:i + 1]))
                        own.wait()
                        dve.wait_ge(turned, t * 2 + 1)
                        nc.vector.tensor_scalar(xn_t[:, i, :], x_t[:, slot + i, :], mv[:, i, 0:1], rstd[:, i:i + 1],
                                                ALU.subtract, ALU.mult).then_inc(normed, 1)

                with dve.Fori(0, NT // NX) as m:
                    for slot in range(0, NX, 2):
                        pair(m * NX + slot, m, slot)
                pair(NT - 2, NT // NX, 0)
                with dve.Fori(0, NTOK // QB // 2) as n2:
                    for i in range(2):
                        for m in range(3):
                            dve.wait_ge(qc_done, n2 * 6 + (3 * i + m + 1))
                            if m == 0:
                                dve.wait_ge(qc_out[i], n2 * 16 + 16)
                            nc.vector.tensor_copy(qc_t[:, i, m, :], qc_ps[m][:, 0:QB]).then_inc(qc_copied, 1)

            @block.tensor
            def _(pe):
                pe.sem_inc(turned, 1)
                with pe.Fori(0, NT // 2) as t2:
                    for i in range(2):
                        pe.wait_ge(normed, t2 * 2 + (i + 1))
                        for g in range(2):
                            pe.wait_ge(turned_copied, t2 * 4 + (2 * i + g if i else 1))
                            for f in range(4):
                                c = g * 4 + f
                                mm = nc.tensor.transpose(turn_ps[g][:, f, :], xn_t[:, i, c * P:(c + 1) * P], ident[:])
                            mm.then_inc(turned, 1)
                pe.wait_ge(w_in, 16)
                pe.wait_ge(turned_copied, NT * 2 + 1)
                with pe.Fori(0, NTOK // QB) as n:
                    for m in range(3):
                        pe.wait_ge(qc_copied, n * 3 + 1)
                        for f in range(FC):
                            mm = nc.tensor.matmul(qc_ps[m][:, 0:QB], w_dq[:, f, m * P:(m + 1) * P],
                                                  xnT[:, f, bass.ds(n * QB, QB)], start=(f == 0), stop=(f == FC - 1))
                        mm.then_inc(qc_done, 1)

            @block.scalar
            def _(act):
                act.sem_inc(turned_copied, 1)
                with act.Fori(0, NT // 2) as t2:
                    for i in range(2):
                        act.wait_ge(var_ready, t2 * 2 + (i + 1))
                        nc.scalar.activation(std[:, i:i + 1], var[:, i:i + 1], ACT.Sqrt).then_inc(std_ready, 1)
                    for i in range(2):
                        for g in range(2):
                            act.wait_ge(turned, t2 * 4 + (2 * i + g + 2))
                            nc.scalar.copy(xnT[:, g * 4:g * 4 + 4, bass.ds(t2 * (2 * P) + i * P, P)], turn_ps[g][:]).then_inc(turned_copied, 1)


def attend_stage(nc, a, ident, ahead, ahead_in, kv_rows, qc_dram, o_dram):
    with ExitStack() as ctx:
        sb = lambda name, shape, dt=F32: ctx.enter_context(nc.sbuf_tensor(name, shape, dt))
        ps = lambda name, shape: ctx.enter_context(nc.psum_tensor(name, shape, F32))
        sem = lambda name: ctx.enter_context(nc.semaphore(name))
        NG_BUF = 4
        w_uq, w_qr, w_ukT, w_uv = ahead
        qc_t = sb("a_qc_t", [P, 3, LQ])
        q_nope = sb("q_nope", [P, 2, LQ])
        q_lat = [sb(f"q_lat{i}", [P, 2, LQ, H]) for i in range(2)]
        q_rot2 = sb("q_rot2", [2 * R, LQ, H])
        q_rot = [q_rot2[0:R], q_rot2[R:2 * R]]
        o_lat = sb("o_lat", [P, 2, H, LQ])
        o_t = sb("o_t", [P, 2, 2, LQ])
        qcos = sb("qcos", [2 * R, LQ])
        qsin = sb("qsin", [2 * R, LQ])
        by_cos = sb("by_cos", [2 * R, LQ])
        by_sin = sb("by_sin", [2 * R, LQ])
        window_i = sb("window_i", [P, GROUPS], I32)
        rows_i = sb("rows_i", [RW, 2 * GROUPS], I32)
        base = sb("base", [P, GROUPS])
        back = sb("back", [P, 1])
        keep = sb("keep", [P, 1])
        place_f = sb("place_f", [P, GROUPS])
        place = sb("place", [P, GROUPS], U32)
        place_of = sb("place_of", [P, NG_BUF], U32)
        seg_f = sb("seg_f", [RW, 2 * GROUPS])
        ma = sb("ma", [RW, SL])
        mb = sb("mb", [RW, SL])
        mc = sb("mc", [RW, SL])
        mask = sb("mask", [RW, 2, 2, SL])
        kv = sb("kv", [P, NG_BUF, KW])
        kvT = sb("kvT", [P, 2, P])
        krT2 = sb("krT2", [2 * R, P])
        krT = [krT2[0:R], krT2[R:2 * R]]
        score = sb("score", [RW, 2, 2, SL])
        top = sb("top", [RW, 2, 2])
        total = sb("total", [RW, 2, 2])
        share = sb("share", [RW, 2, 2])
        prob = sb("prob", [RW, 2, 2, SL])
        probT = sb("probT", [P, RW])
        nope_ps = ps("nope_ps", [P, 512])
        rot_ps = ps("rot_ps", [P, 512])
        lat_ps = ps("lat_ps", [P, 2, 256])
        turn_ps = ps("a_turn_ps", [P, 4, P])
        score_ps = ps("score_ps", [P, 512])
        probT_ps = ps("probT_ps", [P, 512])
        mix_ps = [ps(f"mix_ps{i}", [P, 2, 256]) for i in range(2)]

        consts_in = sem("a_consts_in")
        qc_in = sem("a_qc_in")
        nope_done, nope_read = sem("a_nope_done"), sem("a_nope_read")
        rot_done, rot_read = sem("a_rot_done"), sem("a_rot_read")
        lat_done, lat_read = sem("a_lat_done"), sem("a_lat_read")
        place_ready = sem("a_place_ready")
        kv_in = [sem(f"a_kv_in{i}") for i in range(NG_BUF)]
        turn_done, turn_read = sem("a_turn_done"), sem("a_turn_read")
        score_done, score_read = sem("a_score_done"), sem("a_score_read")
        mask_ready = sem("a_mask_ready")
        top_ready = sem("a_top_ready")
        exp_done = sem("a_exp_done")
        prob_ready = sem("a_prob_ready")
        probT_done, probT_read = sem("a_probT_done"), sem("a_probT_read")
        mix_done, mix_read = sem("a_mix_done"), sem("a_mix_read")
        o_out = [sem(f"a_o_out{i}") for i in range(2)]
        rot_own, soft_own, pool_own, set_own = sem("a_rot_own"), sem("a_soft_own"), sem("a_pool_own"), sem("a_set_own")
        HUV = H // 2

        def steps(eng, step):
            step(None, 0, 0, 0)
            with eng.Fori(0, BATCH // 2 - 1) as i:
                step(i * 2, i * 2 + 1, 0, 1)
                step(i * 2 + 1, i * 2 + 2, 1, 0)
            step(BATCH - 2, BATCH - 1, 0, 1)
            step(BATCH - 1, None, 1, 0)

        def heads_before(bg, bh):
            return (bh + 1) * H if bh is not None else (bg + 1) * H

        with nc.Block() as block:
            @block.sync
            def _(sp):
                sp.dma_start(qc_t[:], qc_dram[:, :, 0:LQ]).then_inc(qc_in, 16)
                for dst, src in ((window_i, "window"), (rows_i, "seg_rows"), (base, "base"), (back, "back"), (keep, "keep"),
                                 (ma, "ma"), (mb, "mb"), (mc, "mc"), (qcos, "qcos"), (qsin, "qsin")):
                    sp.dma_start(dst[:], a[src]).then_inc(consts_in, 16)
                for i in range(2):
                    sp.sem_inc(o_out[i], 16)

                def step(bg, bh, pg, ph):
                    if bh is not None and bg is None:
                        sp.wait_ge(rot_done, H)
                        sp.dma_start(qc_t[:], qc_dram[:, :, LQ:2 * LQ]).then_inc(qc_in, 16)
                        return
                    if bh is not None:
                        sp.wait_ge(rot_done, (bh + 1) * H + bg * HUV)
                        nxt = (bh + 1) * LQ if not isinstance(bh, int) or bh + 1 < BATCH else None
                        if nxt is not None:
                            sp.dma_start(qc_t[:], qc_dram[:, :, bass.ds(nxt, LQ)]).then_inc(qc_in, 16)
                    for q in range(HUV):
                        sp.wait_ge(nope_read, heads_before(bg, bh) + bg * HUV + (q + 2))
                        sp.wait_ge(rot_read, heads_before(bg, bh) + bg * HUV + (q + 2))
                        sp.dma_start(o_dram[:, 2 * q:2 * q + 2, bass.ds(bg * LQ, LQ)], o_t[:, q % 2]).then_inc(o_out[q % 2], 16)

                steps(sp, step)
                for i in range(2):
                    sp.wait_ge(o_out[i], 16 * (BATCH * HUV // 2 + 1))

            @block.gpsimd
            def _(pool):
                pool.wait_ge(place_ready, 1)
                gather_rows = kv_rows
                with pool.Fori(0, GROUPS // NG_BUF) as g4:
                    own = Count(pool, pool_own, g4 * (4 * NG_BUF))
                    for k in range(NG_BUF):
                        pool.wait_ge(mix_done, g4 * NG_BUF + (k + 1))
                        own.mark(pool.tensor_copy(place_of[:, k:k + 1], place[:, bass.ds(g4 * NG_BUF + k, 1)]))
                        own.wait()
                        pool.wait_ge(score_read, g4 * NG_BUF + (k + 1))
                        m = mask[:, k % 2]
                        wide = lambda t: t[:].unsqueeze(1).to_broadcast([RW, 2, SL])
                        seg = seg_f[:, bass.ds(g4 * (2 * NG_BUF) + 2 * k, 2)].unsqueeze(2).to_broadcast([RW, 2, SL])
                        own.mark(pool.tensor_tensor(m, wide(ma), seg, ALU.add))
                        pool.indirect_dma_start(kv[:, k, :], None, gather_rows,
                                                bass.IndirectOffsetOnAxis(place_of[:, k:k + 1], 0)).then_inc(kv_in[k], 16)
                        own.wait()
                        own.mark(pool.tensor_tensor(m, m, m, ALU.mult))
                        own.wait()
                        own.mark(pool.tensor_tensor(m, m, wide(mb), ALU.mult))
                        own.wait()
                        pool.tensor_tensor(m, m, wide(mc), ALU.add).then_inc(mask_ready, 1)

            @block.tensor
            def _(pe):
                pe.sem_inc(mix_done, NG_BUF)
                pe.wait_ge(ahead_in, 16 * 4 * BATCH)
                pe.wait_ge(qc_in, 16)

                def step(bg, bh, pg, ph):
                    uv0 = 0 if bg is None else bg * HUV
                    first = 0 if bg is None else bg * NG

                    def head(u):
                        n = bh * H + u
                        pe.wait_ge(nope_read, n + uv0 + 1)
                        for k in range(3):
                            mm = nc.tensor.matmul(nope_ps[:, 0:LQ], w_uq[:, k, u * HD:(u + 1) * HD], qc_t[:, k, :],
                                                  start=(k == 0), stop=(k == 2))
                        mm.then_inc(nope_done, 1)

                    def pair_rotary(v):
                        pe.wait_ge(rot_read, bh * H + 2 * v + uv0 + 1)
                        for k in range(3):
                            mm = nc.tensor.matmul(rot_ps[:, 0:LQ], w_qr[:, k, v * 2 * R:(v + 1) * 2 * R], qc_t[:, k, :],
                                                  start=(k == 0), stop=(k == 2))
                        mm.then_inc(rot_done, 2)

                    def head_latent(u):
                        n = bh * H + u
                        pe.wait_ge(nope_read, n + uv0 + 2)
                        pe.wait_ge(lat_read, n + 1)
                        for k in range(2):
                            mm = nc.tensor.matmul(lat_ps[:, k, 0:LQ], w_ukT[:, u, k * P:(k + 1) * P], q_nope[:, u % 2, :],
                                                  start=True, stop=True)
                        mm.then_inc(lat_done, 1)

                    def turn(u):
                        n = first + u
                        pe.wait_ge(kv_in[u % NG_BUF], bg * (16 * NG // NG_BUF) + 16 * (u // NG_BUF + 1))
                        pe.wait_ge(turn_read, n + 1)
                        for k in range(2):
                            nc.tensor.transpose(turn_ps[:, k, :], kv[:, u % NG_BUF, k * P:(k + 1) * P], ident[:])
                        nc.tensor.transpose(turn_ps[0:R, 2, :], kv[:, u % NG_BUF, KVC:KW], ident[:]).then_inc(turn_done, 1)

                    def scores(u):
                        n = first + u
                        pe.wait_ge(turn_read, n + 2)
                        pe.wait_ge(score_read, n + 2)
                        if u == 0:
                            pe.wait_ge(lat_read, (bg + 1) * H + 1)
                            pe.wait_ge(rot_read, (bg + 1) * H + bg * HUV + 1)
                        for s in range(2):
                            q0 = u * GQ + s * QS
                            o = score_ps[0:RW, s * SL:(s + 1) * SL]
                            for k in range(2):
                                nc.tensor.matmul(o, q_lat[pg][:, k, q0:q0 + QS, :].rearrange("p q h -> p (q h)"),
                                                 kvT[:, k, s * SL:(s + 1) * SL], start=(k == 0), stop=False)
                            mm = nc.tensor.matmul(o, q_rot[pg][:, q0:q0 + QS, :].rearrange("p q h -> p (q h)"),
                                                  krT[pg][:, s * SL:(s + 1) * SL], start=False, stop=True)
                        mm.then_inc(score_done, 1)

                    def turn_probs(u):
                        n = first + u
                        pe.wait_ge(prob_ready, n + 1)
                        pe.wait_ge(probT_read, n + 1)
                        nc.tensor.transpose(probT_ps[:, 0:RW], prob[:, u % 2].rearrange("p s c -> p (s c)"),
                                            ident[0:RW, 0:RW]).then_inc(probT_done, 1)

                    def mix(u):
                        n = first + u
                        pe.wait_ge(probT_read, n + 2)
                        pe.wait_ge(mix_read, n + 1)
                        for s in range(2):
                            for k in range(2):
                                mm = nc.tensor.matmul(mix_ps[s][:, k, 0:RW], kv[s * SL:(s + 1) * SL, u % NG_BUF, k * P:(k + 1) * P],
                                                      probT[s * SL:(s + 1) * SL, :], start=True, stop=True)
                        mm.then_inc(mix_done, 1)

                    if bh is not None and bg is not None:
                        pe.wait_ge(qc_in, bh * 16 + 16)
                    for u in range(H + 2 if bg is not None else H + 1):
                        if bh is not None and u < H:
                            head(u)
                        if bg is not None and u >= 2:
                            turn_probs(u - 2)
                        if bh is not None and u < H and u % 2:
                            pair_rotary(u // 2)
                        elif bh is not None and 1 <= u < H + 1:
                            head_latent(u - 1)
                        if bg is not None:
                            if 1 <= u < NG + 1:
                                scores(u - 1)
                            if u >= 2:
                                mix(u - 2)
                            if u < NG:
                                turn(u)
                        if bh is not None and u < H and u % 2:
                            head_latent(u - 1)
                    if bg is None:
                        return
                    pe.wait_ge(mix_read, first + (NG + 1))
                    for h in range(H):
                        bank, done, read = ((nope_ps, nope_done, nope_read), (rot_ps, rot_done, rot_read))[h % 2]
                        pe.wait_ge(read, heads_before(bg, bh) + uv0 + (h // 2 + 1))
                        for k in range(2):
                            mm = nc.tensor.matmul(bank[:, 0:LQ], w_uv[:, k, h * HD:(h + 1) * HD], o_lat[:, k, h, :],
                                                  start=(k == 0), stop=(k == 1))
                        mm.then_inc(done, 1)

                steps(pe, step)

            @block.scalar
            def _(act):
                act.sem_inc(nope_read, 1)
                act.sem_inc(lat_read, 1)
                act.sem_inc(mix_read, 1)

                def step(bg, bh, pg, ph):
                    uv0 = 0 if bg is None else bg * HUV
                    first = 0 if bg is None else bg * NG

                    def latent(w):
                        act.wait_ge(lat_done, bh * H + (w + 1))
                        nc.scalar.copy(q_lat[ph][:, :, :, w], lat_ps[:, :, 0:LQ]).then_inc(lat_read, 1)

                    for u in range(H + 2 if bg is not None else H + 1):
                        if bh is not None and u < H:
                            act.wait_ge(nope_done, bh * H + uv0 + (u + 1))
                            nc.scalar.copy(q_nope[:, u % 2, :], nope_ps[:, 0:LQ]).then_inc(nope_read, 1)
                        if bh is not None and 1 <= u < H + 1 and u % 2 == 0:
                            latent(u - 1)
                        if bg is not None and 1 <= u < NG + 1:
                            w = u - 1
                            act.wait_ge(top_ready, first + (w + 1))
                            for s in range(2):
                                ex = nc.scalar.activation(prob_raw(w)[:, s, :], score[:, w % 2, s, :], ACT.Exp,
                                                          bias=top[:, w % 2, s:s + 1], scale=SCALE,
                                                          accum_out=total[:, w % 2, s:s + 1])
                            ex.then_inc(exp_done, 1)
                        if bg is not None and u >= 2:
                            w = u - 2
                            act.wait_ge(mix_done, first + (w + 1 + NG_BUF))
                            for s in range(2):
                                q0 = w * GQ + s * QS
                                cp = nc.scalar.copy(o_lat[:, :, :, q0:q0 + QS].rearrange("p k h q -> p k q h"),
                                                    mix_ps[s][:, :, 0:RW].rearrange("p k (q h) -> p k q h", h=H))
                            cp.then_inc(mix_read, 1)
                        if bh is not None and u < H and u % 2:
                            latent(u - 1)
                    if bg is None:
                        return
                    for q in range(HUV):
                        act.wait_ge(nope_done, heads_before(bg, bh) + uv0 + (q + 1))
                        act.wait_ge(o_out[q % 2], bg * (16 * HUV // 2) + 16 * (q // 2 + 1))
                        nc.scalar.copy(o_t[:, q % 2, 0, :], nope_ps[:, 0:LQ]).then_inc(nope_read, 1)

                def prob_raw(w):
                    return score[:, w % 2]

                steps(act, step)

            @block.vector
            def _(dve):
                dve.sem_inc(rot_read, 1)
                dve.sem_inc(turn_read, 1)
                dve.sem_inc(score_read, 2)
                dve.sem_inc(probT_read, 1)
                dve.wait_ge(consts_in, 16 * 10)
                own = Count(dve, set_own)
                own.mark(nc.vector.tensor_copy(place_f[:], window_i[:]))
                own.mark(nc.vector.tensor_copy(seg_f[:], rows_i[:]))
                own.wait()
                own.mark(nc.vector.tensor_scalar(place_f[:], place_f[:], -1000.0, 2000.0, ALU.max, ALU.min))
                own.mark(nc.vector.tensor_scalar(seg_f[:], seg_f[:], -1000.0, 2000.0, ALU.max, ALU.min))
                own.wait()
                own.mark(nc.vector.tensor_scalar(place_f[:], place_f[:], back[:], 0.0, ALU.add, ALU.max))
                own.wait()
                own.mark(nc.vector.tensor_scalar(place_f[:], place_f[:], float(LK - 1), keep[:], ALU.min, ALU.mult))
                own.wait()
                nc.vector.tensor_tensor(place[:], place_f[:], base[:], ALU.add).then_inc(place_ready, 1)

                def step(bg, bh, pg, ph):
                    uv0 = 0 if bg is None else bg * HUV
                    first = 0 if bg is None else bg * NG
                    rot = Count(dve, rot_own, bh * (5 * H // 2)) if bh is not None else None
                    soft = Count(dve, soft_own, bg * (2 * NG)) if bg is not None else None
                    for u in range(H + 2 if bg is not None else H + 1):
                        if bg is not None and u >= 2:
                            w = u - 2
                            dve.wait_ge(exp_done, first + (w + 1))
                            soft.mark(nc.vector.reciprocal(share[:, w % 2], total[:, w % 2]))
                            soft.wait()
                            nc.vector.tensor_tensor(prob[:, w % 2], score[:, w % 2],
                                                    share[:, w % 2].unsqueeze(2).to_broadcast([RW, 2, SL]),
                                                    ALU.mult).then_inc(prob_ready, 1)
                            dve.wait_ge(probT_done, first + (w + 1))
                            dve.wait_ge(mix_done, first + (w + NG_BUF))
                            nc.vector.tensor_copy(probT[:], probT_ps[:, 0:RW]).then_inc(probT_read, 1)
                        if bh is not None and 2 <= u < H + 1 and u % 2 == 0:
                            v = u // 2 - 1
                            rot.wait()
                            nc.vector.tensor_tensor(q_rot[ph][:, :, 2 * v], by_cos[0:R], by_sin[0:R], ALU.add)
                            nc.vector.tensor_tensor(q_rot[ph][:, :, 2 * v + 1], by_cos[R:2 * R], by_sin[R:2 * R],
                                                    ALU.add).then_inc(rot_read, 2)
                        if bg is not None and 1 <= u < NG + 1:
                            w = u - 1
                            dve.wait_ge(score_done, first + (w + 1))
                            dve.wait_ge(mask_ready, first + (w + 1))
                            nc.vector.scalar_tensor_tensor(
                                score[:, w % 2].rearrange("p s c -> p (s c)"), mask[:, w % 2].rearrange("p s c -> p (s c)"), 0.0,
                                score_ps[0:RW, 0:2 * SL], ALU.min, ALU.add).then_inc(score_read, 1)
                            dve.wait_ge(score_read, first + (w + 3))
                            soft.mark(nc.vector.tensor_reduce(share[:, w % 2], score[:, w % 2], AX_X, ALU.max))
                            soft.wait()
                            nc.vector.tensor_scalar(top[:, w % 2], share[:, w % 2], -SCALE, None,
                                                    ALU.mult).then_inc(top_ready, 1)
                        if bh is not None and u < H and u % 2:
                            v, hf = u // 2, R // 2
                            dve.wait_ge(rot_done, bh * H + uv0 + (2 * v + 2))
                            rot.mark(nc.vector.tensor_tensor(by_cos[:], rot_ps[:, 0:LQ], qcos[:], ALU.mult))
                            for to in range(4):
                                at, of = slice(to * hf, (to + 1) * hf), slice((to ^ 1) * hf, ((to ^ 1) + 1) * hf)
                                rot.mark(nc.vector.tensor_tensor(by_sin[at], rot_ps[of, 0:LQ], qsin[of], ALU.mult))
                        if bg is not None and u < NG:
                            dve.wait_ge(turn_done, first + (u + 1))
                            if u:
                                dve.wait_ge(score_done, first + u)
                            nc.vector.tensor_copy(kvT[:], turn_ps[:, 0:2, :])
                            nc.vector.tensor_copy(krT[pg], turn_ps[0:R, 2, :]).then_inc(turn_read, 1)
                    if bg is None:
                        return
                    for q in range(HUV):
                        dve.wait_ge(rot_done, heads_before(bg, bh) + uv0 + (q + 1))
                        dve.wait_ge(o_out[q % 2], bg * (16 * HUV // 2) + 16 * (q // 2 + 1))
                        nc.vector.tensor_copy(o_t[:, q % 2, 1, :], rot_ps[:, 0:LQ]).then_inc(rot_read, 1)

                steps(dve, step)


def project_stage(nc, a, ident, gates, logits, squares, o_dram, xn_rows, out):
    with ExitStack() as ctx:
        sb = lambda name, shape, dt=F32: ctx.enter_context(nc.sbuf_tensor(name, shape, dt))
        ps = lambda name, shape: ctx.enter_context(nc.psum_tensor(name, shape, F32))
        sem = lambda name: ctx.enter_context(nc.semaphore(name))
        w_hi = sb("w_o_hi", [P, H, D], F32R)
        w_lo = sb("w_o_lo", [P, H, D], F32R)
        router = sb("router", [P, FC, E])
        router_scale = sb("router_scale", [P, FC])
        o_t = sb("p_o_t", [P, H, P])
        o_hi = sb("p_o_hi", [P, 2, H, P], F32R)
        o_lo = sb("p_o_lo", [P, 2, H, P], F32R)
        x1_t = sb("x1_t", [P, 2, D])
        xn_t = sb("p_xn_t", [P, 2, D])
        xnT = sb("p_xnT", [P, FC, P])
        sq = sb("p_sq", [P, D])
        spare_t = sb("p_spare_t", [P, D])
        w_stage = [spare_t[:], sq[:], xn_t[:, 0], xn_t[:, 1]]
        NS = len(w_stage)
        zeros = sb("p_zeros", [P, D])
        stats = sb("p_stats", [P, 2, 6])
        mv = sb("p_mv", [P, 2])
        spare = sb("p_spare", [P, 1])
        var = sb("p_var", [P, 1])
        std = sb("p_std", [P, 1])
        rstd = sb("p_rstd", [P, 1])
        attn_ps = [[ps(f"attn_ps{i}{h}", [P, 512]) for h in range(2)] for i in range(2)]
        turn_ps = [ps(f"p_turn_ps{i}", [P, 4, P]) for i in range(2)]
        logit_ps = ps("logit_ps", [P, 512])

        w_in = [sem(f"p_w_in{i}") for i in range(NS)]
        w_hi_done, w_lo_done = sem("p_w_hi_done"), sem("p_w_lo_done")
        o_hi_done, o_lo_done = sem("p_o_hi_done"), sem("p_o_lo_done")
        consts_in = sem("p_consts_in")
        o_in = sem("p_o_in")
        x_in = [sem(f"p_x_in{i}") for i in range(2)]
        attn_done = sem("p_attn_done")
        x1_half = sem("p_x1_half")
        var_ready = sem("p_var_ready")
        std_ready = sem("p_std_ready")
        normed = sem("p_normed")
        turned, turned_copied = sem("p_turned"), sem("p_turned_copied")
        logits_done, logits_read = sem("p_logits_done"), sem("p_logits_read")
        scaled = sem("p_scaled")
        zeroed = sem("p_zeroed")
        rows_out = [sem(f"p_rows_out{i}") for i in range(2)]
        fill_out = sem("p_fill_out")
        own_sem = sem("p_dve_own")
        out_rows = out.rearrange("(t h) c -> t (h c)", h=2)

        LAST = NT // 2 - 1

        with nc.Block() as block:
            @block.sync
            def _(sp):
                sp.sem_inc(rows_out[0], 32)
                sp.sem_inc(rows_out[1], 32)
                sp.dma_start(router[:], a["router"]).then_inc(consts_in, 16)
                sp.dma_start(router_scale[:], a["router_scale"]).then_inc(consts_in, 16)
                sp.dma_start(o_t[:], o_dram[:, :, 0:P]).then_inc(o_in, 16)
                for k in range(H):
                    if k >= NS:
                        sp.wait_ge(w_lo_done, k - NS + 1)
                    sp.dma_start(w_stage[k % NS], a["w_o"][:, k]).then_inc(w_in[k % NS], 16)
                    if k == 1:
                        sp.wait_ge(o_lo_done, 1)
                        sp.dma_start(o_t[:], o_dram[:, :, P:2 * P]).then_inc(o_in, 16)
                for i in range(2):
                    sp.dma_start(x1_t[:, i], a["x"][i]).then_inc(x_in[i], 16)
                sp.wait_ge(o_lo_done, 2)
                sp.dma_start(o_t[:], o_dram[:, :, 2 * P:3 * P]).then_inc(o_in, 16)
                sp.wait_ge(zeroed, 1)
                sp.dma_start(out_rows[NTOK:, :], zeros[:]).then_inc(fill_out, 16)

                def tile(t, i, m, more, more_o):
                    sp.wait_ge(normed, t + 1)
                    sp.dma_start(out_rows[bass.ds(t * P, P), :], x1_t[:, i]).then_inc(rows_out[i], 16)
                    sp.dma_start(xn_rows[bass.ds(t * P, P), :], xn_t[:, i]).then_inc(rows_out[i], 16)
                    if more_o:
                        sp.wait_ge(o_lo_done, t + 3)
                        sp.dma_start(o_t[:], o_dram[:, :, bass.ds((t + 3) * P, P)]).then_inc(o_in, 16)
                    if more:
                        sp.wait_ge(rows_out[i], m * 32 + 64)
                        sp.dma_start(x1_t[:, i], a["x"][t + 2]).then_inc(x_in[i], 16)

                with sp.Fori(0, LAST - 1) as j:
                    tile(j * 2, 0, j, True, True)
                    tile(j * 2 + 1, 1, j, True, True)
                tile(NT - 4, 0, LAST - 1, True, True)
                tile(NT - 3, 1, LAST - 1, True, False)
                tile(NT - 2, 0, LAST, False, False)
                tile(NT - 1, 1, LAST, False, False)
                for i in range(2):
                    sp.wait_ge(rows_out[i], 32 * (NT // 2 + 1))
                sp.wait_ge(fill_out, 16)

            @block.gpsimd
            def _(pool):
                pool.memset(zeros[:], 0.0).then_inc(zeroed, 1)

            @block.tensor
            def _(pe):
                pe.wait_ge(scaled, FC)

                def share(i, k, h):
                    cut = slice(h * 512, (h + 1) * 512)
                    return split_product(nc, attn_ps[i][h][:], (o_hi[:, i, k, :], o_lo[:, i, k, :]),
                                         (w_hi[:, k, cut], w_lo[:, k, cut]), k == 0, k == H - 1)

                def first_two():
                    pe.wait_ge(o_lo_done, 2)
                    for k in range(H):
                        pe.wait_ge(w_lo_done, k + 1)
                        for i in range(2):
                            for h in range(2):
                                mm = share(i, k, h)
                            if k == H - 1:
                                mm.then_inc(attn_done, 1)

                def attn(t, i):
                    pe.wait_ge(o_lo_done, t + 1)
                    pe.wait_ge(x1_half, t * 2 + 1)
                    for k in range(H):
                        if k == H // 2:
                            turn(t - 1, 1 - i)
                        for h in range(2):
                            mm = share(i, k, h)
                    mm.then_inc(attn_done, 1)

                def turn(t, i):
                    pe.wait_ge(normed, t + 1)
                    for g in range(2):
                        pe.wait_ge(turned_copied, t * 2 + (g + 1))
                        for f in range(4):
                            c = g * 4 + f
                            mm = nc.tensor.transpose(turn_ps[g][:, f, :], xn_t[:, i, c * P:(c + 1) * P], ident[:])
                        mm.then_inc(turned, 1)

                def route(t):
                    pe.wait_ge(turned_copied, t * 2 + 4)
                    pe.wait_ge(logits_read, t + 1)
                    for f in range(FC):
                        mm = nc.tensor.matmul(logit_ps[:, 0:E], xnT[:, f, :], router[:, f, :], start=(f == 0), stop=(f == FC - 1))
                    mm.then_inc(logits_done, 1)

                pe.sem_inc(logits_done, 1)
                first_two()
                turn(0, 0)
                route(0)
                with pe.Fori(0, LAST) as j:
                    attn(j * 2 + 2, 0)
                    route(j * 2 + 1)
                    attn(j * 2 + 3, 1)
                    route(j * 2 + 2)
                turn(NT - 1, 1)
                route(NT - 1)

            @block.vector
            def _(dve):
                dve.sem_inc(x1_half, 3)
                dve.sem_inc(logits_read, 1)
                dve.wait_ge(consts_in, 32)
                for f in range(FC):
                    nc.vector.tensor_scalar(router[:, f, :], router[:, f, :], router_scale[:, f:f + 1], None,
                                            ALU.mult).then_inc(scaled, 1)

                def norm(t, i, m):
                    own = Count(dve, own_sem, t * 4)
                    dve.wait_ge(attn_done, t + 1)
                    dve.wait_ge(x_in[i], m * 16 + 16)
                    dve.wait_ge(rows_out[i], m * 32 + 32)
                    for h in range(2):
                        cut = slice(h * 512, (h + 1) * 512)
                        nc.vector.scalar_tensor_tensor(x1_t[:, i, cut], attn_ps[i][h][:], gates[:, 0:1], x1_t[:, i, cut],
                                                       ALU.mult, ALU.add).then_inc(x1_half, 1)
                    dve.wait_ge(x1_half, t * 2 + 5)
                    for h in range(2):
                        own.mark(nc.vector.bn_stats(stats[:, h, :], x1_t[:, i, h * 512:(h + 1) * 512]))
                    own.wait()
                    nc.vector.tensor_copy(spare[:], stats[:, 0, 0:1])
                    own.mark(nc.vector.bn_aggr(mv[:], stats[:]))
                    own.wait()
                    nc.vector.tensor_scalar(var[:], mv[:, 1:2], LN_EPS, None, ALU.add).then_inc(var_ready, 1)
                    dve.wait_ge(std_ready, t + 1)
                    own.mark(nc.vector.reciprocal(rstd[:], std[:]))
                    own.wait()
                    nc.vector.tensor_scalar(xn_t[:, i, :], x1_t[:, i, :], mv[:, 0:1], rstd[:],
                                            ALU.subtract, ALU.mult).then_inc(normed, 1)

                def o_low(t, i):
                    dve.wait_ge(o_hi_done, t + 1)
                    nc.vector.tensor_tensor(o_lo[:, i], o_t[:], o_hi[:, i], ALU.subtract).then_inc(o_lo_done, 1)

                def keep_logits(t):
                    dve.wait_ge(logits_done, t + 2)
                    nc.vector.tensor_copy(logits[:, bass.ds(t, 1), :].rearrange("p t e -> p (t e)"),
                                          logit_ps[:, 0:E]).then_inc(logits_read, 1)

                def pair(j, more):
                    norm(j * 2 + 1, 1, j)
                    o_low(j * 2 + 3, 1)
                    keep_logits(j * 2)
                    norm(j * 2 + 2, 0, j + 1)
                    if more:
                        o_low(j * 2 + 4, 0)
                    keep_logits(j * 2 + 1)

                o_low(0, 0)
                for k in range(H):
                    if k == 2:
                        o_low(1, 1)
                    dve.wait_ge(w_hi_done, k + 1)
                    nc.vector.tensor_tensor(w_lo[:, k, :], w_stage[k % NS], w_hi[:, k, :], ALU.subtract).then_inc(w_lo_done, 1)
                dve.wait_ge(w_lo_done, H)
                norm(0, 0, 0)
                o_low(2, 0)
                with dve.Fori(0, LAST - 1) as j:
                    pair(j, True)
                pair(LAST - 1, False)
                norm(NT - 1, 1, LAST)
                keep_logits(NT - 2)
                keep_logits(NT - 1)

            @block.scalar
            def _(act):
                act.sem_inc(turned_copied, 2)

                def root(t):
                    act.wait_ge(var_ready, t + 1)
                    nc.scalar.activation(std[:], var[:], ACT.Sqrt).then_inc(std_ready, 1)

                def finish(t, i):
                    act.wait_ge(normed, t + 1)
                    nc.scalar.activation(sq[:], xn_t[:, i, :], ACT.Square,
                                         accum_out=squares[:, bass.ds(t, 1)])
                    for g in range(2):
                        act.wait_ge(turned, t * 2 + (g + 1))
                        act.wait_ge(logits_done, t + 1)
                        nc.scalar.copy(xnT[:, g * 4:g * 4 + 4, :], turn_ps[g][:]).then_inc(turned_copied, 1)

                def o_high(t, i):
                    act.wait_ge(o_in, t * 16 + 16)
                    if not isinstance(t, int) or t > 1:
                        act.wait_ge(attn_done, t - 1)
                    nc.scalar.copy(o_hi[:, i], o_t[:]).then_inc(o_hi_done, 1)

                def pair(j, more):
                    finish(j * 2, 0)
                    root(j * 2 + 1)
                    o_high(j * 2 + 3, 1)
                    finish(j * 2 + 1, 1)
                    root(j * 2 + 2)
                    if more:
                        o_high(j * 2 + 4, 0)

                o_high(0, 0)
                for k in range(H):
                    if k == 2:
                        o_high(1, 1)
                    act.wait_ge(w_in[k % NS], 16 * (k // NS + 1))
                    nc.scalar.copy(w_hi[:, k, :], w_stage[k % NS]).then_inc(w_hi_done, 1)
                root(0)
                o_high(2, 0)
                with act.Fori(0, LAST - 1) as j:
                    pair(j, True)
                pair(LAST - 1, False)
                finish(NT - 2, 0)
                root(NT - 1)
                finish(NT - 1, 1)


def route_stage(nc, a, gates, logits, squares, supers, slot_info):
    with ExitStack() as ctx:
        sb = lambda name, shape, dt=F32: ctx.enter_context(nc.sbuf_tensor(name, shape, dt))
        ps = lambda name, shape: ctx.enter_context(nc.psum_tensor(name, shape, F32))
        sem = lambda name: ctx.enter_context(nc.semaphore(name))
        W = [P, NT, E]
        scale = sb("expert_scale", [P, E])
        before = sb("before", [P, P])
        ones = sb("ones", [P, P])
        iota_e = sb("iota_e", [P, E])
        steps = sb("steps", [P, NT])
        sup_steps = sb("sup_steps", [P, 3])
        iota_s = sb("iota_s", [P, NSUP])
        info = sb("info", [P, 2, NT, 2])
        rms = sb("r_rms", [P, NT])
        root = sb("r_root", [P, NT])
        lg, low, prob = sb("lg", W), sb("low", W), sb("r_prob", W)
        tmp, coef, both = sb("r_tmp", W), sb("r_coef", W), sb("r_both", W)
        hot = [sb(f"hot{k}", W) for k in range(2)]
        pick = sb("pick", [P, NT])
        best = sb("best", [P, NT])
        norm = sb("r_norm", [P, NT])
        part = sb("r_part", [P, NT])
        rank, tot, pre = sb("rank", W), sb("tot", W), sb("pre", W)
        cnt, tiles, sups = sb("cnt", [P, E]), sb("tiles", [P, E]), sb("sups", [P, E])
        tile0, sup0, row0 = sb("tile0", [P, E]), sb("sup0", [P, E]), sb("row0", [P, E])
        over = sb("over", [P, E, NT])
        slot = sb("slot", [P, 2, NT], U32)
        SW = [1, NSUP, E]
        s_hot, s_rel, s_tmp = sb("s_hot", SW), sb("s_rel", SW), sb("s_tmp", SW)
        s_f = sb("s_f", [1, NSUP + 1, 4])
        rank_ps, tot_ps = ps("rank_ps", [P, 512]), ps("tot_ps", [P, 512])
        consts_in, own_sem = sem("r_consts_in"), sem("r_own")
        ms_ready, root_ready, diff_ready, exp_ready = sem("r_ms"), sem("r_root_ready"), sem("r_diff"), sem("r_exp")
        both_ready, ranked, info_ready, scattered = sem("r_both_ready"), sem("r_ranked"), sem("r_info"), sem("r_scattered")
        over_e = lambda t: t[:].unsqueeze(2).to_broadcast(W)
        over_t = lambda t: t[:].unsqueeze(1).to_broadcast(W)

        with nc.Block() as block:
            @block.sync
            def _(sp):
                for dst, src in ((scale, "expert_scale"), (before, "before"), (ones, "ones"), (iota_e, "iota_e"),
                                 (steps, "steps"), (sup_steps, "sup_steps"), (iota_s, "iota_s")):
                    sp.dma_start(dst[:], a[src]).then_inc(consts_in, 16)
                for k in range(2):
                    sp.dma_start(info[:, k, :, 0], a["token"], allow_slow_non_contiguous=True).then_inc(consts_in, 16)

            @block.scalar
            def _(act):
                act.wait_ge(ms_ready, 1)
                nc.scalar.activation(root[:], rms[:], ACT.Sqrt).then_inc(root_ready, 1)
                act.wait_ge(diff_ready, 1)
                nc.scalar.activation(prob[:], tmp[:], ACT.Exp).then_inc(exp_ready, 1)

            @block.tensor
            def _(pe):
                pe.wait_ge(consts_in, 16 * 9)
                pe.wait_ge(both_ready, 1)
                flat = both[:].rearrange("p t e -> p (t e)")
                nc.tensor.matmul(rank_ps[:, 0:NT * E], before[:], flat, start=True, stop=True)
                nc.tensor.matmul(tot_ps[:, 0:NT * E], ones[:], flat, start=True, stop=True).then_inc(ranked, 1)

            @block.gpsimd
            def _(pool):
                pool.wait_ge(info_ready, 1)
                for k in range(2):
                    for t in range(NT):
                        pool.indirect_dma_start(slot_info, bass.IndirectOffsetOnAxis(slot[:, k, t:t + 1], 0),
                                                info[:, k, t, :], None).then_inc(scattered, 16)
                pool.wait_ge(scattered, 16 * 2 * NT)

            @block.vector
            def _(dve):
                own = Count(dve, own_sem)

                def do(ins):
                    own.mark(ins)
                    own.wait()

                v = nc.vector
                v.tensor_scalar(rms[:], squares[:], 1.0 / D, RMS_EPS, ALU.mult, ALU.add).then_inc(ms_ready, 1)
                dve.wait_ge(root_ready, 1)
                do(v.reciprocal(rms[:], root[:]))
                do(v.tensor_scalar(rms[:], rms[:], float(D) ** -0.5, None, ALU.mult))
                do(v.tensor_tensor(lg[:], logits[:], over_e(rms), ALU.mult))
                dve.wait_ge(consts_in, 16 * 9)
                for k in range(2):
                    src = lg if k == 0 else low
                    do(v.tensor_reduce(best[:], src[:], AX_X, ALU.max))
                    if k == 0:
                        v.tensor_tensor(tmp[:], lg[:], over_e(best), ALU.subtract).then_inc(diff_ready, 1)
                    do(v.tensor_tensor(coef[:], src[:], over_e(best), ALU.is_lt))
                    do(v.scalar_tensor_tensor(coef[:], coef[:], 100.0, over_t(iota_e), ALU.mult, ALU.add))
                    do(v.tensor_reduce(pick[:], coef[:], AX_X, ALU.min))
                    do(v.tensor_tensor(hot[k][:], over_t(iota_e), over_e(pick), ALU.is_equal))
                    if k == 0:
                        do(v.scalar_tensor_tensor(low[:], hot[0][:], -1e30, lg[:], ALU.mult, ALU.add))
                v.tensor_tensor(both[:], hot[0][:], hot[1][:], ALU.add).then_inc(both_ready, 1)
                dve.wait_ge(both_ready, 1)
                dve.wait_ge(exp_ready, 1)
                do(v.tensor_reduce(norm[:], prob[:], AX_X, ALU.add))
                do(v.reciprocal(norm[:], norm[:]))
                do(v.tensor_tensor(prob[:], prob[:], over_e(norm), ALU.mult))
                do(v.tensor_tensor(tmp[:], prob[:], both[:], ALU.mult))
                do(v.tensor_reduce(norm[:], tmp[:], AX_X, ALU.add))
                do(v.scalar_tensor_tensor(norm[:], norm[:], 0.0, norm[:], ALU.is_le, ALU.add))
                do(v.reciprocal(norm[:], norm[:]))
                do(v.tensor_tensor(coef[:], prob[:], over_t(scale), ALU.mult))
                do(v.tensor_tensor(coef[:], coef[:], over_e(norm), ALU.mult))
                do(v.tensor_scalar(coef[:], coef[:], gates[:, 1:2], None, ALU.mult))
                dve.wait_ge(ranked, 1)
                do(v.tensor_copy(tot[:], tot_ps[:, 0:NT * E].rearrange("p (t e) -> p t e", e=E)))
                do(v.tensor_copy(rank[:], rank_ps[:, 0:NT * E].rearrange("p (t e) -> p t e", e=E)))
                do(v.memset(pre[:, 0, :], 0.0))
                for t in range(1, NT):
                    do(v.tensor_tensor(pre[:, t, :], pre[:, t - 1, :], tot[:, t - 1, :], ALU.add))
                do(v.tensor_tensor(cnt[:], pre[:, NT - 1, :], tot[:, NT - 1, :], ALU.add))
                do(v.tensor_tensor(over[:], cnt[:].unsqueeze(2).to_broadcast([P, E, NT]),
                                   steps[:].unsqueeze(1).to_broadcast([P, E, NT]), ALU.is_gt))
                do(v.tensor_reduce(tiles[:], over[:], AX_X, ALU.add))
                do(v.tensor_tensor(over[:, :, 0:3], tiles[:].unsqueeze(2).to_broadcast([P, E, 3]),
                                   sup_steps[:].unsqueeze(1).to_broadcast([P, E, 3]), ALU.is_gt))
                do(v.tensor_reduce(sups[:], over[:, :, 0:3], AX_X, ALU.add))
                for first, size in ((tile0, tiles), (sup0, sups)):
                    do(v.memset(first[:, 0:1], 0.0))
                    for e in range(1, E):
                        do(v.tensor_tensor(first[:, e:e + 1], first[:, e - 1:e], size[:, e - 1:e], ALU.add))
                do(v.tensor_scalar(row0[:], tile0[:], float(P), None, ALU.mult))
                do(v.tensor_tensor(rank[:], rank[:], pre[:], ALU.add))
                do(v.tensor_tensor(rank[:], rank[:], over_t(row0), ALU.add))
                for k in range(2):
                    do(v.tensor_tensor(tmp[:], hot[k][:], rank[:], ALU.mult))
                    do(v.tensor_reduce(part[:], tmp[:], AX_X, ALU.add))
                    do(v.tensor_copy(slot[:, k, :], part[:]))
                    do(v.tensor_tensor(tmp[:], hot[k][:], coef[:], ALU.mult))
                    do(v.tensor_reduce(info[:, k, :, 1], tmp[:], AX_X, ALU.add))
                v.memset(s_f[:], 0.0).then_inc(info_ready, 1)
                dve.wait_ge(info_ready, 1)
                se = lambda t: t[0:1, :].unsqueeze(1).to_broadcast(SW)
                ss = iota_s[0:1, :].unsqueeze(2).to_broadcast(SW)
                do(v.tensor_tensor(s_rel[:], ss, se(sup0), ALU.subtract))
                do(v.tensor_tensor(s_hot[:], s_rel[:], se(sups), ALU.is_lt))
                do(v.tensor_scalar(s_tmp[:], s_rel[:], 0.0, None, ALU.is_ge))
                do(v.tensor_tensor(s_hot[:], s_hot[:], s_tmp[:], ALU.mult))
                do(v.tensor_scalar(s_rel[:], s_rel[:], float(ST), None, ALU.mult))
                do(v.tensor_tensor(s_tmp[:], s_hot[:], se(iota_e), ALU.mult))
                do(v.tensor_reduce(s_f[:, 0:NSUP, 0], s_tmp[:], AX_X, ALU.add))
                do(v.tensor_tensor(s_tmp[:], se(tiles), s_rel[:], ALU.subtract))
                do(v.tensor_tensor(s_tmp[:], s_tmp[:], s_hot[:], ALU.mult))
                do(v.tensor_reduce(s_f[:, 0:NSUP, 1], s_tmp[:], AX_X, ALU.add))
                do(v.tensor_scalar(s_f[:, 0:NSUP, 1], s_f[:, 0:NSUP, 1], float(ST), None, ALU.min))
                do(v.tensor_tensor(s_tmp[:], se(tile0), s_rel[:], ALU.add))
                do(v.tensor_tensor(s_tmp[:], s_tmp[:], s_hot[:], ALU.mult))
                do(v.tensor_reduce(s_f[:, 0:NSUP, 2], s_tmp[:], AX_X, ALU.add))
                do(v.tensor_copy(s_f[:, 1:NSUP + 1, 3], s_f[:, 0:NSUP, 2]))
                do(v.tensor_copy(supers[:], s_f[:]))


def experts_stage(nc, a, ident, supers, slot_info, xn_rows, out):
    with ExitStack() as ctx:
        sb = lambda name, shape, dt=F32: ctx.enter_context(nc.sbuf_tensor(name, shape, dt))
        ps = lambda name, shape: ctx.enter_context(nc.psum_tensor(name, shape, F32))
        sem = lambda name: ctx.enter_context(nc.semaphore(name))
        NC_UP, NC = 4, 6
        HC = HID // NC_UP
        NR, HF = 3, FC // 2
        w_raw = [sb(f"w_raw{i}", [P, HF, 512]) for i in range(NR)]
        w_hi = [sb(f"w_hi{i}", [P, FC, 512], F32R) for i in range(2)]
        w_lo = [sb(f"w_lo{i}", [P, FC, 512], F32R) for i in range(2)]
        info = sb("e_info", [P, ST, 2])
        coef = sb("e_coef", [P, ST])
        token = sb("e_token", [P, ST], U32)
        place = sb("e_place", [P, 2, ST], U32)
        x_t = sb("e_x_t", [P, ST, D])
        xT_hi = sb("e_xT_hi", [P, ST, FC, P], F32R)
        xT_lo = sb("e_xT_lo", [P, ST, FC, P], F32R)
        hid = sb("e_hid", [P, ST, HC])
        hidT_hi = sb("e_hidT_hi", [P, ST, FC, P], F32R)
        hidT_lo = sb("e_hidT_lo", [P, ST, FC, P], F32R)
        y = sb("e_y", [P, 4, 512])
        spare = sb("e_spare", [P, 32])
        warm = sb("e_warm", [P, 1])
        unit_ps = [ps(f"unit_ps{i}", [P, 512]) for i in range(4)]
        turn_ps = [ps(f"e_turn_ps{i}", [P, 4, P]) for i in range(2)]
        hidT_ps = ps("hidT_ps", [P, 2, P])

        w_in = [sem(f"e_w_in{i}") for i in range(NR)]
        w_hi_done, w_lo_done = sem("e_w_hi_done"), sem("e_w_lo_done")
        xT_hi_done, hidT_hi_done = sem("e_xT_hi_done"), sem("e_hidT_hi_done")
        info_in, info_used = sem("e_info_in"), sem("e_info_used")
        x_in = [sem(f"e_x_in{t}") for t in range(ST)]
        turned, turned_copied = sem("e_turned"), sem("e_turned_copied")
        unit_done, unit_read = sem("e_unit_done"), sem("e_unit_read")
        gelu_ready = sem("e_gelu_ready")
        hidT_done, hidT_copied = sem("e_hidT_done"), sem("e_hidT_copied")
        y_added, y_free = sem("e_y_added"), sem("e_y_free")
        pool_own, spare_set, warmed = sem("e_pool_own"), sem("e_spare_set"), sem("e_warmed")
        spot = lambda c, t: 2 * (c % 2) + t % 2

        def read(eng, s, col, top):
            return eng.value_load(supers[0:1, bass.ds(s, 1), col:col + 1].rearrange("p s c -> p (s c)"), min_val=0, max_val=top)

        with nc.Block() as block:
            @block.sync
            def _(sp):
                def load_info(s):
                    sp.dma_start(info[:], slot_info[bass.ds(read(sp, s, 2, MAXT) * P, ST * P), :]
                                 .rearrange("(t p) c -> p t c", p=P)).then_inc(info_in, 16)

                load_info(0)
                with sp.Fori(0, NSUP) as s:
                    n = read(sp, s, 1, ST)
                    e = read(sp, s, 0, E - 1)
                    more = read(sp, s + 1, 1, ST)
                    with sp.If(n > 0):
                        for j in range(2 * NC):
                            c = j // 2
                            sp.wait_ge(w_lo_done, s * (2 * NC) + (j + 1))
                            src = a["gate_up"][e * NC_UP + c] if c < NC_UP else a["linear"][e * 2 + (c - NC_UP)]
                            sp.dma_start(w_raw[j % NR][:], src[:, (j % 2) * HF:(j % 2 + 1) * HF, :]).then_inc(w_in[j % NR], 16)
                        with sp.If(more > 0):
                            sp.wait_ge(info_used, s * 3 + 3)
                            load_info(s + 1)
                        sp.wait_ge(info_used, 3)

            @block.gpsimd
            def _(pool):
                pool.sem_inc(y_free, 2)

                places = iter(range(1, 32))

                def carry():
                    at = next(places)
                    return pool.tensor_tensor(spare[:, at:at + 1], spare[:, 0:1], spare[:, 0:1], ALU.add)

                def gather(s, base):
                    own = Count(pool, pool_own, base)
                    pool.wait_ge(info_in, s * 16 + 16)
                    carry()
                    own.mark(pool.tensor_copy(token[:], info[:, :, 0]))
                    own.wait()
                    carry()
                    for t in range(ST):
                        pool.indirect_dma_start(x_t[:, t, :], None, xn_rows,
                                                bass.IndirectOffsetOnAxis(token[:, t:t + 1], 0)).then_inc(x_in[t], 16)

                pool.memset(spare[:], 0.0).then_inc(spare_set, 1)
                pool.wait_ge(spare_set, 1)
                gather(0, 0)
                with pool.Fori(0, NSUP) as s:
                    n, first = read(pool, s, 1, ST), read(pool, s, 2, MAXT)
                    more = read(pool, s + 1, 1, ST)
                    with pool.If(n > 0):
                        pool.wait_ge(info_in, s * 16 + 16)
                        for t in range(ST):
                            pool.wait_ge(x_in[t], s * 16 + 16)
                        carry()
                        pool.tensor_scalar(place[:, 0, :], info[:, :, 0], 2.0, None, ALU.mult).then_inc(info_used, 1)
                        pool.tensor_scalar(place[:, 1, :], info[:, :, 0], 2.0, 1.0, ALU.mult, ALU.add).then_inc(info_used, 1)
                        pool.wait_ge(info_used, s * 3 + 3)
                        carry()
                        with pool.If(more > 0):
                            pool.wait_ge(turned, (first + n) * 2)
                            gather(s + 1, s + 1)
                        for c in range(2):
                            for t in range(ST):
                                unit = first * 2 + n * c + t
                                with pool.If(n > t):
                                    pool.wait_ge(unit_read, first * NC + n * (NC_UP + c) + (t + 3))
                                    carry()
                                    pool.indirect_dma_start(out, bass.IndirectOffsetOnAxis(place[:, c, t:t + 1], 0),
                                                            y[:, spot(c, t), :], None,
                                                            compute_op=ALU.add).then_inc(y_added, 16)
                                    pool.wait_ge(y_added, unit * 16 + 16)
                                    carry().then_inc(y_free, 1)
                                pool.wait_ge(spare_set, 1)

            @block.tensor
            def _(pe):
                pe.sem_inc(unit_done, 1)

                def turn_x(s, first, t):
                    pe.wait_ge(x_in[t], s * 16 + 16)
                    for g in range(2):
                        pe.wait_ge(turned_copied, first * 2 + (2 * t + g + 1))
                        for f in range(4):
                            k = g * 4 + f
                            mm = nc.tensor.transpose(turn_ps[g][:, f, :], x_t[:, t, k * P:(k + 1) * P], ident[:])
                        mm.then_inc(turned, 1)

                turn_x(0, 0, 0)
                with pe.Fori(0, NSUP) as s:
                    n, first = read(pe, s, 1, ST), read(pe, s, 2, MAXT)
                    more = read(pe, s + 1, 1, ST)
                    turn = lambda t: turn_x(s, first, t)

                    def unit(c, t, turn_next=None):
                        if t == 0:
                            pe.wait_ge(w_lo_done, s * (2 * NC) + (2 * c + 2 + NR))
                        if c == 0:
                            pe.wait_ge(turned_copied, (first + t) * 2 + 4)
                        if c == NC_UP:
                            pe.wait_ge(hidT_copied, first * 4 + n * 3 + (t + 2))
                        pe.wait_ge(unit_read, first * NC + n * c + (t + 1))
                        left_hi, left_lo = (xT_hi, xT_lo) if c < NC_UP else (hidT_hi, hidT_lo)
                        for k in range(FC):
                            if k == FC // 2 and turn_next is not None and t + 1 < ST:
                                with pe.If(n > t + 1):
                                    turn_next(t + 1)
                                pe.wait_ge(x_in[0], 16)
                            mm = split_product(nc, unit_ps[spot(c, t)][:], (left_hi[:, t, k, :], left_lo[:, t, k, :]),
                                               (w_hi[c % 2][:, k, :], w_lo[c % 2][:, k, :]), k == 0, k == FC - 1)
                        mm.then_inc(unit_done, 1)

                    def turn_hidden(c, t):
                        pe.wait_ge(unit_read, first * NC + n * c + (t + 3))
                        pe.wait_ge(hidT_copied, first * 4 + n * c + (t + 1))
                        for k in range(2):
                            mm = nc.tensor.transpose(hidT_ps[:, k, :], hid[:, t, k * P:(k + 1) * P], ident[:])
                        mm.then_inc(hidT_done, 1)

                    with pe.If(n > 0):
                        for t in range(ST):
                            with pe.If(n > t):
                                unit(0, t, turn)
                            pe.wait_ge(x_in[0], 16)
                        for c in range(1, NC_UP):
                            for t in range(ST):
                                with pe.If(n > t):
                                    turn_hidden(c - 1, t)
                                    unit(c, t)
                                pe.wait_ge(x_in[0], 16)
                        turn_hidden(NC_UP - 1, 0)
                        for t in range(ST):
                            with pe.If(n > t):
                                unit(NC_UP, t, lambda r: turn_hidden(NC_UP - 1, r))
                            pe.wait_ge(x_in[0], 16)
                        with pe.If(more > 0):
                            turn_x(s + 1, first + n, 0)
                        pe.wait_ge(x_in[0], 16)
                        for t in range(ST):
                            with pe.If(n > t):
                                unit(NC_UP + 1, t)
                            pe.wait_ge(x_in[0], 16)

            @block.scalar
            def _(act):

                def split_high(s, c, h, free):
                    j = 2 * c + h
                    act.wait_ge(w_in[j % NR], s * (16 * 2 * NC // NR) + 16 * (j // NR + 1))
                    if h == 0:
                        act.wait_ge(unit_done, free)
                    nc.scalar.copy(w_hi[c % 2][:, h * HF:(h + 1) * HF, :], w_raw[j % NR][:]).then_inc(w_hi_done, 1)

                nc.scalar.activation(warm[:], ident[:, 0:1], ACT.Gelu_apprx_tanh).then_inc(warmed, 1)
                for h in range(2):
                    split_high(0, 0, h, 1)

                def keep_x_of(first, t):
                    for g in range(2):
                        act.wait_ge(turned, first * 2 + (2 * t + g + 1))
                        nc.scalar.copy(xT_hi[:, t, 4 * g:4 * g + 4, :], turn_ps[g][:]).then_inc(xT_hi_done, 1)

                keep_x_of(0, 0)
                with act.Fori(0, NSUP) as s:
                    n, first = read(act, s, 1, ST), read(act, s, 2, MAXT)
                    more = read(act, s + 1, 1, ST)

                    def gate(c, t):
                        act.wait_ge(unit_done, first * NC + n * c + (t + 2))
                        nc.scalar.activation(hid[:, t, :], unit_ps[spot(c, t)][:, 0:HC],
                                             ACT.Gelu_apprx_tanh).then_inc(gelu_ready, 1)

                    def keep(c, t):
                        act.wait_ge(hidT_done, first * 4 + n * c + (t + 1))
                        nc.scalar.copy(hidT_hi[:, t, 2 * c:2 * c + 2, :], hidT_ps[:]).then_inc(hidT_hi_done, 1)

                    keep_x = lambda t: keep_x_of(first, t)

                    with act.If(n > 0):
                        act.wait_ge(warmed, s + 1)
                        nc.scalar.activation(warm[:], ident[:, 0:1], ACT.Gelu_apprx_tanh).then_inc(warmed, 1)
                        for c in range(NC_UP + 1):
                            for t in range(ST):
                                if c == 0 and t + 1 < ST:
                                    with act.If(n > t + 1):
                                        keep_x(t + 1)
                                    act.wait_ge(unit_done, 1)
                                with act.If(n > t):
                                    if c:
                                        keep(c - 1, t)
                                    if c < NC_UP:
                                        gate(c, t)
                                act.wait_ge(unit_done, 1)
                                if t < 2:
                                    split_high(s, c + 1, t, first * NC + n * c + 1)
                        with act.If(more > 0):
                            keep_x_of(first + n, 0)
                            for h in range(2):
                                split_high(s + 1, 0, h, first * NC + n * (NC - 1) + 1)
                        act.wait_ge(unit_done, 1)

            @block.vector
            def _(dve):
                dve.sem_inc(turned_copied, 2)
                dve.sem_inc(unit_read, 2)
                dve.sem_inc(hidT_copied, 1)
                dve.sem_inc(w_lo_done, NR)

                def split_low(s, c, h):
                    j = 2 * c + h
                    dve.wait_ge(w_hi_done, s * (2 * NC) + (j + 1))
                    nc.vector.tensor_tensor(w_lo[c % 2][:, h * HF:(h + 1) * HF, :], w_raw[j % NR][:],
                                            w_hi[c % 2][:, h * HF:(h + 1) * HF, :], ALU.subtract).then_inc(w_lo_done, 1)

                for h in range(2):
                    split_low(0, 0, h)

                def keep_x_of(first, t):
                    for g in range(2):
                        dve.wait_ge(xT_hi_done, first * 2 + (2 * t + g + 1))
                        nc.vector.tensor_tensor(xT_lo[:, t, 4 * g:4 * g + 4, :], turn_ps[g][:],
                                                xT_hi[:, t, 4 * g:4 * g + 4, :], ALU.subtract).then_inc(turned_copied, 1)

                keep_x_of(0, 0)
                with dve.Fori(0, NSUP) as s:
                    n, first = read(dve, s, 1, ST), read(dve, s, 2, MAXT)
                    more = read(dve, s + 1, 1, ST)

                    keep_x = lambda t: keep_x_of(first, t)

                    def keep_hidden(c, t):
                        dve.wait_ge(hidT_hi_done, first * 4 + n * c + (t + 1))
                        nc.vector.tensor_tensor(hidT_lo[:, t, 2 * c:2 * c + 2, :], hidT_ps[:],
                                                hidT_hi[:, t, 2 * c:2 * c + 2, :], ALU.subtract).then_inc(hidT_copied, 1)

                    def times_up(c, t):
                        dve.wait_ge(gelu_ready, first * 4 + n * c + (t + 1))
                        nc.vector.tensor_tensor(hid[:, t, :], hid[:, t, :], unit_ps[spot(c, t)][:, HC:2 * HC],
                                                ALU.mult).then_inc(unit_read, 1)

                    def weigh(c, t):
                        unit = first * 2 + n * c + t
                        dve.wait_ge(unit_done, first * NC + n * (NC_UP + c) + (t + 2))
                        dve.wait_ge(y_free, unit + 1)
                        nc.vector.tensor_scalar(y[:, spot(c, t), :], unit_ps[spot(NC_UP + c, t)][:], coef[:, t:t + 1], None,
                                                ALU.mult).then_inc(unit_read, 1)

                    with dve.If(n > 0):
                        dve.wait_ge(info_in, s * 16 + 16)
                        dve.wait_ge(unit_read, first * NC + 2)
                        nc.vector.tensor_copy(coef[:], info[:, :, 1]).then_inc(info_used, 1)
                        for t in range(ST):
                            if t + 1 < ST:
                                with dve.If(n > t + 1):
                                    keep_x(t + 1)
                                dve.wait_ge(info_in, 16)
                            with dve.If(n > t):
                                times_up(0, t)
                            dve.wait_ge(info_in, 16)
                            if t < 2:
                                split_low(s, 1, t)
                        for c in range(1, NC_UP):
                            for t in range(ST):
                                with dve.If(n > t):
                                    keep_hidden(c - 1, t)
                                    times_up(c, t)
                                dve.wait_ge(info_in, 16)
                                if t < 2:
                                    split_low(s, c + 1, t)
                        keep_hidden(NC_UP - 1, 0)
                        for t in range(ST):
                            if t + 1 < ST:
                                with dve.If(n > t + 1):
                                    keep_hidden(NC_UP - 1, t + 1)
                                dve.wait_ge(info_in, 16)
                            with dve.If(n > t):
                                weigh(0, t)
                            dve.wait_ge(info_in, 16)
                            if t < 2:
                                split_low(s, NC - 1, t)
                        with dve.If(more > 0):
                            keep_x_of(first + n, 0)
                        dve.wait_ge(info_in, 16)
                        for t in range(ST):
                            with dve.If(n > t):
                                weigh(1, t)
                            dve.wait_ge(info_in, 16)
                            if t < 2:
                                with dve.If(more > 0):
                                    split_low(s + 1, 0, t)
                                dve.wait_ge(info_in, 16)


def layout(x, ctx_2048, itok_BxS_0_1023, g_xattn, g_ffn, L0_xattn_W_kvc, L0_xattn_W_dq, L0_xattn_W_uq, L0_xattn_W_qr,
           L0_xattn_W_uk, L0_xattn_W_kr, L0_xattn_W_uv, L0_xattn_W_o, L0_ffn_router_logits, L0_ffn_gating_einsum,
           L0_ffn_linear, L0_ffn_per_expert_scale, L0_ffn_router_scale):
    n = lambda v: np.asarray(v)
    c = np.ascontiguousarray
    f32 = np.float32
    rows = lambda w: c(n(w).reshape(-1, P, w.shape[-1]).transpose(1, 0, 2))
    half = R // 2
    freq = (1.0 / 10000.0 ** (np.arange(half, dtype=f32) / f32(half))).astype(f32)
    angle = lambda m: np.arange(m, dtype=f32)[:, None] * freq
    seg = n(itok_BxS_0_1023).reshape(NTOK)

    r = np.arange(P) % SL
    is_mean = r == SL - 1
    q_of = np.where(is_mean, 0, (np.arange(P) // SL) * QS + r // WIN)
    groups = np.arange(GROUPS)
    window = c(seg.reshape(GROUPS, GQ)[:, q_of].T)
    back = np.where(is_mean, 0, r % WIN - BACK).astype(f32)[:, None]
    keep = np.where(is_mean, 0.0, 1.0).astype(f32)[:, None]
    batch_of = groups // NG
    base = np.where(is_mean[:, None], BATCH * LK + batch_of, LK * batch_of).astype(f32)

    row_q = np.arange(RW) // H
    col = np.arange(SL)
    mean_col = col == SL - 1
    own = (row_q[:, None] == (col // WIN)[None]) & ~mean_col
    mid = (LK - 1) / 2
    span = (LK - 1 + BACK) / 2
    big = 1e30
    ma = np.where(own, (col % WIN - BACK)[None] - mid, np.where(mean_col[None], -span, 0.0)).astype(f32)
    mb = np.where(own, -big, np.where(mean_col[None], big, 0.0)).astype(f32) + np.zeros((RW, 1), f32)
    mc = np.where(own, big * (mid + 0.5) ** 2, np.where(mean_col[None], -big * (span + 0.5) ** 2, -big)).astype(f32)
    ks, qs = angle(LK), angle(LQ)
    both = lambda t: np.concatenate([t, t], axis=1)
    gw = n(L0_ffn_gating_einsum).reshape(E, 2, 4, HID // 4, FC, P)
    lw = n(L0_ffn_linear).reshape(E, FC, P, 2, F // 2)
    wk = n(L0_xattn_W_kvc)
    fill = np.zeros((SLOTS, 2), f32)
    fill[:, 0] = NTOK + np.arange(SLOTS) % P
    return dict(
        x=n(x).reshape(NT, P, D),
        ctxT=c(n(ctx_2048).reshape(BATCH, KT, KN, FC, P).transpose(0, 1, 4, 3, 2)).reshape(BATCH * KT, P, FC, KN),
        w_kvc=rows(wk), w_kvcT=rows(c(wk.T)), w_kr=rows(L0_xattn_W_kr), w_dq=rows(L0_xattn_W_dq),
        w_uq=rows(L0_xattn_W_uq), w_qr=rows(L0_xattn_W_qr),
        w_ukT=c(n(L0_xattn_W_uk).reshape(KVC, H, HD).transpose(2, 1, 0)),
        w_uv=rows(L0_xattn_W_uv), w_o=rows(L0_xattn_W_o),
        window=window, seg_rows=c(np.repeat(seg.reshape(2 * GROUPS, QS).T, H, axis=0)),
        back=back, keep=keep, base=c(base), ma=ma, mb=mb, mc=mc,
        kcos=c(both(np.cos(ks)).astype(f32).reshape(KT, KN, R).transpose(1, 0, 2)),
        ksin=c(both(np.sin(ks)).astype(f32).reshape(KT, KN, R).transpose(1, 0, 2)),
        qcos=c(np.tile(np.cos(qs), (1, 4)).astype(f32).T),
        qsin=c(np.tile(np.concatenate([np.sin(qs), -np.sin(qs)], axis=1), (1, 2)).astype(f32).T),
        ident=np.eye(P, dtype=f32), inv=np.full((KN, 1), 1.0 / LK, f32),
        gates=np.repeat(np.concatenate([n(g_xattn), n(g_ffn)])[None], P, axis=0),
        router=rows(L0_ffn_router_logits), router_scale=c(n(L0_ffn_router_scale).reshape(FC, P).T),
        expert_scale=np.repeat(n(L0_ffn_per_expert_scale)[None], P, axis=0),
        before=np.triu(np.ones((P, P), f32), 1), ones=np.ones((P, P), f32),
        token=c(np.arange(NTOK, dtype=f32).reshape(NT, P).T),
        gate_up=c(gw.transpose(0, 2, 5, 4, 1, 3)).reshape(E * 4, P, FC, 2 * HID // 4),
        linear=c(lw.transpose(0, 3, 2, 1, 4)).reshape(E * 2, P, FC, F // 2),
        slot_fill=fill, iota_e=np.repeat(np.arange(E, dtype=f32)[None], P, axis=0),
        steps=np.repeat(P * np.arange(NT, dtype=f32)[None], P, axis=0),
        sup_steps=np.repeat(ST * np.arange(3, dtype=f32)[None], P, axis=0),
        iota_s=np.repeat(np.arange(NSUP, dtype=f32)[None], P, axis=0),
    )


def kernel(**inputs):
    import numpy as _np
    import concourse.bacc as _bacc
    from concourse import mybir as _mybir
    from concourse.bass_utils import run_bass_kernel_spmd as _run

    arrays = {f"in_{k}": _np.ascontiguousarray(v) for k, v in layout(**inputs).items()}
    nc = _bacc.Bacc("TRN2", target_bir_lowering=False, num_devices=1)
    a = {k[3:]: nc.dram_tensor(k, v.shape, _mybir.dt.from_np(v.dtype), kind="ExternalInput").ap() for k, v in arrays.items()}
    out = nc.dram_tensor("out", (2 * (NTOK + P), D // 2), F32, kind="ExternalOutput").ap()
    program(nc, a, out)
    r = _run(nc, [arrays], core_ids=[0])
    return r.results[0]["out"][:2 * NTOK].reshape(BATCH, LQ, D)
```
